# Optimizing a Trainium2 kernel written in Bass

```python
import numpy as np
import jax
import jax.numpy as jnp

def _softmax(x, axis=-1):
    return jax.nn.softmax(x, axis=axis)

def _gelu(x):
    return jax.nn.gelu(x, approximate=True)

def _silu(x):
    return jax.nn.silu(x)

def _sigmoid(x):
    return jax.nn.sigmoid(x)

def _layernorm(x, axis=-1, eps=1e-05):
    m = jnp.mean(x, axis=axis, keepdims=True)
    v = jnp.var(x, axis=axis, keepdims=True)
    return (x - m) / jnp.sqrt(v + eps)

def _scatter_add(tgt, idx, src, axis=0):
    return tgt.at[idx].add(src)

def _segment_sum(src, seg, n):
    return jax.ops.segment_sum(src, seg, n)
kernel_name = 'mk_gnn_resnorm_d2_gnn_r8_ecbd0f'

def setup_inputs(seed: int=0):
    np.random.seed(seed)
    _w = jnp.asarray

    def _rec_inputs():
        import jax
        import jax.numpy as jnp
        _gk = jax.random.key(seed)
        x = -0.000202 + 1 * jax.random.normal(jax.random.fold_in(_gk, 1), (12500, 64), jnp.float32)
        src = jax.random.randint(jax.random.fold_in(_gk, 2), (200000,), 0, 12500, jnp.int32)
        dst = jax.random.randint(jax.random.fold_in(_gk, 3), (200000,), 0, 12500, jnp.int32)
        _o = jnp.argsort(dst, stable=True)
        src = src[_o]
        dst = dst[_o]
        edge_attr_64 = 3.07312e-05 + 1.00008 * jax.random.normal(jax.random.fold_in(_gk, 11), (200000, 64), jnp.float32)
        edge_attr_64_n2 = 3.07312e-05 + 1.00008 * jax.random.normal(jax.random.fold_in(_gk, 12), (200000, 64), jnp.float32)
        edge_attr_64_n3 = 3.07312e-05 + 1.00008 * jax.random.normal(jax.random.fold_in(_gk, 13), (200000, 64), jnp.float32)
        return (x, src, dst, edge_attr_64, edge_attr_64_n2, edge_attr_64_n3)
    x, src, dst, edge_attr_64, edge_attr_64_n2, edge_attr_64_n3 = _rec_inputs()

    def _L0_gnn_setup():
        import jax, jax.numpy as jnp
        import numpy as np
        N = 12500
        E = 150000
        IN = 64
        H = 64
        OUT = 64

        def _demo_layer(h, src, dst, deg_pos, inv_deg, Wg, Wl, Ws, b):
            g = h @ Wg
            neigh_mean = jax.ops.segment_sum(h[dst], src, num_segments=h.shape[0]) * inv_deg[:, None]
            extra = neigh_mean @ Wl + h @ Ws
            out = g + deg_pos[:, None] * extra + b
            return jax.nn.elu(out)
        key = jax.random.key(seed)
        ks = jax.random.split(key, 12)
        x = jax.random.normal(ks[0], (N, IN), dtype=jnp.float32)
        edge_index = jax.random.randint(ks[1], (2, E), 0, N)

        def w(k, i, o):
            return jax.random.normal(k, (i, o), dtype=jnp.float32) * (1.0 / np.sqrt(i))
        return {'x': x, 'edge_index': edge_index, 'Wg1': w(ks[2], IN, H), 'Wl1': w(ks[3], IN, H), 'Ws1': w(ks[4], IN, H), 'b1': jnp.zeros((H,), jnp.float32), 'Wg2': w(ks[5], H, H), 'Wl2': w(ks[6], H, H), 'Ws2': w(ks[7], H, H), 'b2': jnp.zeros((H,), jnp.float32), 'Wgo': w(ks[8], H, OUT), 'Wlo': w(ks[9], H, OUT), 'Wso': w(ks[10], H, OUT), 'bo': jnp.zeros((OUT,), jnp.float32)}
    _L0_gnn_all = _L0_gnn_setup()
    _L0_gnn_in = {k: v for k, v in _L0_gnn_all.items() if k in ('Wg1', 'Wl1', 'Ws1', 'b1', 'Wg2', 'Wl2', 'Ws2', 'b2', 'Wgo', 'Wlo', 'Wso', 'bo')}
    del _L0_gnn_all

    def _L1_gnn_setup():
        import jax, jax.numpy as jnp
        import numpy as np
        N_NODES = 12500
        N_EDGES = 62500
        D_NODE = 64
        D_EDGE = 64
        D_TIME = 64
        D_OUT = 64
        key = jax.random.key(seed)
        ks = jax.random.split(key, 10)
        key_dim = D_NODE + D_TIME + D_EDGE
        m2_dim = D_NODE + D_TIME + D_OUT
        return {'node_feature': jax.random.normal(ks[0], (N_NODES, D_NODE), jnp.float32), 'edge_index': jax.random.randint(ks[1], (N_EDGES, 2), 0, N_NODES, jnp.int64), 'edge_feature': jax.random.normal(ks[2], (N_EDGES, D_EDGE), jnp.float32), 'src_time_features': jax.random.normal(ks[3], (N_EDGES, D_TIME), jnp.float32), 'edge_time': jax.random.normal(ks[4], (N_EDGES, D_TIME), jnp.float32), 'W1': jax.random.normal(ks[5], (D_OUT, key_dim), jnp.float32) / np.sqrt(key_dim), 'b1': jnp.zeros((D_OUT,), jnp.float32), 'W2': jax.random.normal(ks[6], (D_OUT, m2_dim), jnp.float32) / np.sqrt(m2_dim), 'b2': jnp.zeros((D_OUT,), jnp.float32)}
    _L1_gnn_all = _L1_gnn_setup()
    _L1_gnn_in = {k: v for k, v in _L1_gnn_all.items() if k in ('W1', 'b1', 'W2', 'b2')}
    del _L1_gnn_all
    return {'x': x, 'src': src, 'dst': dst, 'edge_attr_64': edge_attr_64, 'edge_attr_64_n2': edge_attr_64_n2, 'edge_attr_64_n3': edge_attr_64_n3, 'L0_gnn_Wg1': _L0_gnn_in['Wg1'], 'L0_gnn_Wl1': _L0_gnn_in['Wl1'], 'L0_gnn_Ws1': _L0_gnn_in['Ws1'], 'L0_gnn_b1': _L0_gnn_in['b1'], 'L0_gnn_Wg2': _L0_gnn_in['Wg2'], 'L0_gnn_Wl2': _L0_gnn_in['Wl2'], 'L0_gnn_Ws2': _L0_gnn_in['Ws2'], 'L0_gnn_b2': _L0_gnn_in['b2'], 'L0_gnn_Wgo': _L0_gnn_in['Wgo'], 'L0_gnn_Wlo': _L0_gnn_in['Wlo'], 'L0_gnn_Wso': _L0_gnn_in['Wso'], 'L0_gnn_bo': _L0_gnn_in['bo'], 'L1_gnn_W1': _L1_gnn_in['W1'], 'L1_gnn_b1': _L1_gnn_in['b1'], 'L1_gnn_W2': _L1_gnn_in['W2'], 'L1_gnn_b2': _L1_gnn_in['b2']}

def reference(x, src, dst, edge_attr_64, edge_attr_64_n2, edge_attr_64_n3, L0_gnn_Wg1, L0_gnn_Wl1, L0_gnn_Ws1, L0_gnn_b1, L0_gnn_Wg2, L0_gnn_Wl2, L0_gnn_Ws2, L0_gnn_b2, L0_gnn_Wgo, L0_gnn_Wlo, L0_gnn_Wso, L0_gnn_bo, L1_gnn_W1, L1_gnn_b1, L1_gnn_W2, L1_gnn_b2):
    import jax
    import jax.numpy as jnp

    def _L0_gnn_ref(x, edge_index, Wg1, Wl1, Ws1, b1, Wg2, Wl2, Ws2, b2, Wgo, Wlo, Wso, bo):
        import jax, jax.numpy as jnp
        import numpy as np
        N = 12500
        E = 150000
        IN = 64
        H = 64
        OUT = 64

        def _demo_layer(h, src, dst, deg_pos, inv_deg, Wg, Wl, Ws, b):
            g = h @ Wg
            neigh_mean = jax.ops.segment_sum(h[dst], src, num_segments=h.shape[0]) * inv_deg[:, None]
            extra = neigh_mean @ Wl + h @ Ws
            out = g + deg_pos[:, None] * extra + b
            return jax.nn.elu(out)
        src, dst = (edge_index[0], edge_index[1])
        n = x.shape[0]
        deg = jax.ops.segment_sum(jnp.ones(src.shape[0], x.dtype), src, num_segments=n)
        deg_pos = jnp.where(deg > 0, jnp.float32(1.0), jnp.float32(0.0))
        inv_deg = deg_pos / jnp.maximum(deg, 1.0)
        h = _demo_layer(x, src, dst, deg_pos, inv_deg, Wg1, Wl1, Ws1, b1)
        h = _demo_layer(h, src, dst, deg_pos, inv_deg, Wg2, Wl2, Ws2, b2)
        return _demo_layer(h, src, dst, deg_pos, inv_deg, Wgo, Wlo, Wso, bo)

    def _L1_gnn_ref(node_feature, edge_index, edge_feature, src_time_features, edge_time, W1, b1, W2, b2):
        import jax, jax.numpy as jnp
        import numpy as np
        N_NODES = 12500
        N_EDGES = 62500
        D_NODE = 64
        D_EDGE = 64
        D_TIME = 64
        D_OUT = 64
        N = node_feature.shape[0]
        ei = jnp.concatenate([edge_index, edge_index[:, ::-1]], axis=0)
        ef = jnp.concatenate([edge_feature, edge_feature], axis=0)
        stf = jnp.concatenate([src_time_features, src_time_features], axis=0)
        et = jnp.concatenate([edge_time, edge_time], axis=0)
        time_unit = src_time_features[0:1]
        node_id = jnp.arange(N, dtype=ei.dtype)
        ei = jnp.concatenate([ei, jnp.stack([node_id, node_id], axis=1)], axis=0)
        ef = jnp.concatenate([ef, jnp.zeros((N, ef.shape[1]), ef.dtype)], axis=0)
        stf = jnp.concatenate([stf, jnp.tile(time_unit, (N, 1))], axis=0)
        et = jnp.concatenate([et, jnp.tile(time_unit, (N, 1))], axis=0)
        node_i = ei[:, 0]
        node_j = ei[:, 1]
        src_vec = jnp.concatenate([node_feature[node_i], stf], axis=1)
        seg_sum = jax.ops.segment_sum(src_vec, node_i, num_segments=N)
        cnt = jax.ops.segment_sum(jnp.ones((node_i.shape[0], 1), src_vec.dtype), node_i, num_segments=N)
        source_node_vec = seg_sum / jnp.maximum(cnt, 1.0)
        target_vec = jnp.concatenate([node_feature[node_j], ef, et], axis=1)
        neighbor_emb = target_vec @ W1.T + b1
        neighbors_sum = jax.nn.relu(jax.ops.segment_sum(neighbor_emb, node_i, num_segments=N))
        out = jnp.concatenate([neighbors_sum, source_node_vec], axis=1) @ W2.T + b2
        return out
    edge_index = jnp.stack([src, dst])
    edge_index_t = jnp.stack([src, dst], axis=1)
    x = _layernorm(x + _L0_gnn_ref(x, edge_index, L0_gnn_Wg1, L0_gnn_Wl1, L0_gnn_Ws1, L0_gnn_b1, L0_gnn_Wg2, L0_gnn_Wl2, L0_gnn_Ws2, L0_gnn_b2, L0_gnn_Wgo, L0_gnn_Wlo, L0_gnn_Wso, L0_gnn_bo), axis=-1)
    x = _layernorm(x + _L1_gnn_ref(x, edge_index_t, edge_attr_64, edge_attr_64_n2, edge_attr_64_n3, L1_gnn_W1, L1_gnn_b1, L1_gnn_W2, L1_gnn_b2), axis=-1)
    return x

_drawn_inputs = setup_inputs


def setup_inputs(seed=0):
    import zlib

    import numpy as np

    out = dict(_drawn_inputs(seed))
    spreads = {'L0_gnn_b1': (0.0, 0.1),
     'L0_gnn_b2': (0.0, 0.1),
     'L0_gnn_bo': (0.0, 0.1),
     'L1_gnn_b1': (0.0, 0.1),
     'L1_gnn_b2': (0.0, 0.29)}
    factors = {}
    for name, (base, spread) in spreads.items():
        noise = np.random.default_rng([zlib.crc32(name.encode()), seed]).standard_normal(out[name].shape)
        drawn = base * np.exp(spread * noise) if base else spread * noise
        out[name] = jnp.asarray(drawn.astype(out[name].dtype))
    for name, factor in factors.items():
        out[name] = (out[name] * factor).astype(out[name].dtype)
    return out
```

```python
from contextlib import ExitStack

import numpy as np

import concourse.bass as bass
from concourse import mybir

ALU = mybir.AluOpType
ACT = mybir.ActivationFunctionType
AX = mybir.AxisListType
F32 = mybir.dt.float32
BF16 = mybir.dt.bfloat16
I32 = mybir.dt.int32

P = 128
D = 64
N = 12500
E = 200000
T = -(-N // P)
N_FULL = N // P
N_LAST = N - N_FULL * P
EPS = 1e-5

COLS = E // P
REST = E - COLS * P
LANES = 5
STEPS = -(-(COLS + 1) // LANES)
KEYC = STEPS * LANES
BINS = T + 1

B = 8
CHUNKS = -(-(E // P + T + 1) // (2 * B)) * (2 * B)
BATCHES = CHUNKS // B
ROWS = CHUNKS * P

EF, ET, STF, ONE, LOC_S, ID_D, LOC_D, ID_S, ROW = 0, D, 2 * D, 3 * D, 193, 194, 195, 196, 200
FEAT = ONE + 1
WIDE = FEAT + D

PB = 11
PBATCHES = COLS // PB
ZR = 16
NT = 7
NGROUPS = T // NT
PS = 4

assert COLS % (2 * PB) == 0 and ROWS % (ZR * P) == 0 and T % NT == 0 and B % PS == 0


def build(nc, x, src, dst, ef, stf, et, Wg1, Wl1, Ws1, b1, Wg2, Wl2, Ws2, b2, Wgo, Wlo, Wso, bo,
          W1t, c1, W2t, c2, out):
    with ExitStack() as ctx:
        early = ExitStack()

        def sb(name, shape, dt=F32):
            return ctx.enter_context(nc.sbuf_tensor(name, shape, dt))

        def sb_early(name, shape, dt=F32):
            return early.enter_context(nc.sbuf_tensor(name, shape, dt))

        def sem(name):
            return ctx.enter_context(nc.semaphore(name))

        def dram(name, shape):
            return nc.dram_tensor(name, shape, F32).ap()

        sorted_s = dram("sorted_by_src", (ROWS, ROW))
        sorted_d = dram("sorted_by_dst", (ROWS, ROW))
        h_dram = [None, dram("h1", (T * P, D)), dram("h2", (T * P, D)), dram("x1", (T * P, D))]
        run_wide_s = dram("run_wide_s", ((CHUNKS + 1) * P, WIDE))
        run_wide_d = dram("run_wide_d", ((CHUNKS + 1) * P, WIDE))
        run_thin = [dram(f"run_thin{i}", ((CHUNKS + 1) * P, D)) for i in range(3)]

        ps_seg = ctx.enter_context(nc.psum_tensor("ps_seg", [P, PS, 512], F32))
        ps_t = ctx.enter_context(nc.psum_tensor("ps_t", [P, 8, P], F32))
        ps_o = ctx.enter_context(nc.psum_tensor("ps_o", [P, 8, P], F32))

        iota_bin = sb("iota_bin", [P, BINS], BF16)
        iota_loc = sb("iota_loc", [P, P])
        iota_row = sb("iota_row", [P, P])
        iota_part = sb("iota_part", [P, 1])
        iota_part_i = sb("iota_part_i", [P, 1], I32)
        iota_tmp = sb("iota_tmp", [P, P], I32)
        upper = sb("upper", [P, P], BF16)
        lower = sb("lower", [P, P], BF16)
        ones_bf = sb("ones_bf", [P, P], BF16)
        ones = sb("ones", [P, P])
        ident = sb("ident", [P, P])

        keep = {k: sb(f"keep_{k}", [P, CHUNKS]) for k in "sd"}
        lastrow = {k: sb(f"lastrow_{k}", [P, T], I32) for k in "sd"}
        wts = [sb(f"wts{i}", [P, P]) for i in range(3)]
        bias = [sb(f"bias{i}", [P, D]) for i in range(3)]
        w_n1 = sb("w_n1", [P, D])
        w_n2 = sb("w_n2", [P, P])
        w_n3 = sb("w_n3", [P, D])
        bias_n1 = sb("bias_n1", [P, D])
        bias_n2 = sb("bias_n2", [P, D])
        unit = sb("unit", [P, D])

        iota_chunk_i = sb_early("iota_chunk_i", [P, CHUNKS], I32)
        zeros = sb_early("zeros", [P, ZR * ROW])
        keys = {k: sb_early(f"keys_{k}", [P, KEYC], I32) for k in "sd"}
        tid = {k: sb_early(f"tid_{k}", [P, KEYC], BF16) for k in "sd"}
        pos = {k: sb_early(f"pos_{k}", [P, KEYC]) for k in "sd"}
        meta = sb_early("meta", [P, KEYC, 4], I32)
        onehot = {k: sb_early(f"onehot_{k}", [P, LANES, BINS], BF16) for k in "sd"}
        prod = {k: sb_early(f"prod_{k}", [P, LANES, BINS]) for k in "sd"}
        lane0 = {k: sb_early(f"lane0_{k}", [P, LANES, BINS]) for k in "sd"}
        count = {k: sb_early(f"count_{k}", [P, BINS]) for k in "sd"}
        nchunk = {k: sb_early(f"nchunk_{k}", [P, BINS]) for k in "sd"}
        nchunk_i = {k: sb_early(f"nchunk_i_{k}", [P, BINS], I32) for k in "sd"}
        cend = {k: sb_early(f"cend_{k}", [P, BINS]) for k in "sd"}
        cstart = {k: sb_early(f"cstart_{k}", [P, BINS]) for k in "sd"}
        filled = {k: sb_early(f"filled_{k}", [P, BINS]) for k in "sd"}
        binsq = sb_early("binsq", [P, BINS])
        startcol = {k: sb_early(f"startcol_{k}", [P, 1]) for k in "sd"}
        fillcol = {k: sb_early(f"fillcol_{k}", [P, 1]) for k in "sd"}
        starts = sb_early("starts", [P, CHUNKS])
        prow = sb_early("prow", [P, 2, PB, ROW])
        ppos = sb_early("ppos", [P, 2, 2, PB], I32)
        early.close()

        rows = sb("rows", [P, 2, B, ROW])
        seg_oh = sb("seg_oh", [P, 2, B, P])
        got = sb("got", [P, 2, B, D])
        gidx = sb("gidx", [P, 2, B], I32)
        loc_s = sb("loc_s", [P, CHUNKS + B], I32)
        id_d = sb("id_d", [P, CHUNKS], I32)
        run = sb("run", [P, 2, B, WIDE])
        run_n = run[:, :, :, 0:D]

        h = sb("h", [P, T, D])
        xres = sb("xres", [P, T, D])
        inv = sb("inv", [P, T])
        linked = sb("linked", [P, T])
        nidx = sb("nidx", [P, 3, NT], I32)
        sum_a = sb("sum_a", [P, NT, WIDE])
        sum_b = sb("sum_b", [P, NT, WIDE])
        sum_c = sb("sum_c", [P, NT, D])
        cat = sb("cat", [P, NT, P])
        cat2 = sb("cat2", [P, NT, P])
        catT = sb("catT", [P, 8, P])
        cat2T = sb("cat2T", [P, 8, P])
        na = sb("na", [P, NT, D])
        nb = sb("nb", [P, NT, D])
        nm = sb("nm", [P, NT, 8])
        s_const = sem("s_const")
        s_iota = sem("s_iota")
        s_load = sem("s_load")
        s_wload = sem("s_wload")
        s_xload = sem("s_xload")
        s_hpad = sem("s_hpad")
        s_zero = sem("s_zero")
        s_zrow = sem("s_zrow")
        s_v = sem("s_v")
        s_key = sem("s_key")
        s_oh = {k: sem(f"s_oh_{k}") for k in "sd"}
        s_hist = {k: sem(f"s_hist_{k}") for k in "sd"}
        s_lane0 = {k: sem(f"s_lane0_{k}") for k in "sd"}
        s_rank = {k: sem(f"s_rank_{k}") for k in "sd"}
        s_prod = {k: sem(f"s_prod_{k}") for k in "sd"}
        s_read = {k: sem(f"s_read_{k}") for k in "sd"}
        s_starts = sem("s_starts")
        s_bc = sem("s_bc")
        s_pload = [sem(f"s_pload{i}") for i in range(2)]
        s_pmeta = [sem(f"s_pmeta{i}") for i in range(2)]
        s_pout = [sem(f"s_pout{i}") for i in range(2)]
        s_rest = sem("s_rest")
        s_rmeta = sem("s_rmeta")
        s_rout = sem("s_rout")

        vcount = [0]

        def chain(dve, ins):
            vcount[0] += 1
            ins.then_inc(s_v, 1)
            dve.wait_ge(s_v, vcount[0])

        block = ctx.enter_context(nc.Block())

        class Pass:

            def __init__(self, name, key, table, running, table_rows):
                self.key, self.table, self.running, self.table_rows = key, table, running, table_rows
                self.wide = table_rows is not None
                self.width = WIDE if self.wide else D
                if self.wide:
                    self.row = [sem(f"{name}_row{i}") for i in range(2)]
                else:
                    self.idx = [sem(f"{name}_idx{i}") for i in range(2)]
                if name == "seg1":
                    self.tab = [sem(f"{name}_tab{i}") for i in range(2)]
                self.got = [sem(f"{name}_got{i}") for i in range(2)]
                self.oh = [sem(f"{name}_oh{i}") for i in range(2)]
                self.mm = sem(f"{name}_mm")
                self.run = sem(f"{name}_run")
                self.out = [sem(f"{name}_out{i}") for i in range(2)]

        seg1 = Pass("seg1", "s", x, run_wide_s, sorted_s)
        seg2 = Pass("seg2", "s", h_dram[1], run_thin[0], None)
        seg3 = Pass("seg3", "s", h_dram[2], run_thin[1], None)
        seg4 = Pass("seg4", "s", h_dram[3], run_thin[2], None)
        seg5 = Pass("seg5", "d", h_dram[3], run_wide_d, sorted_d)

        class Nodes:

            def __init__(self, name, number, sums):
                self.number, self.sums = number, sums
                self.idx = sem(f"{name}_idx")
                self.sum = sem(f"{name}_sum")
                self.cat = sem(f"{name}_cat")
                self.tr = sem(f"{name}_tr")
                self.ct = sem(f"{name}_ct")
                self.mm = sem(f"{name}_mm")
                if number == 4:
                    self.cat2 = sem(f"{name}_cat2")
                else:
                    self.neg = sem(f"{name}_neg")
                    self.exp = sem(f"{name}_exp")
                if number >= 3:
                    self.var = sem(f"{name}_var")
                    self.std = sem(f"{name}_std")
                self.v = sem(f"{name}_v")
                self.done = sem(f"{name}_done")
                self.out = sem(f"{name}_out")

        node1 = Nodes("node1", 1, [(run_wide_s, "s", sum_a)])
        node2 = Nodes("node2", 2, [(run_thin[0], "s", sum_c)])
        node3 = Nodes("node3", 3, [(run_thin[1], "s", sum_c)])
        node4 = Nodes("node4", 4, [(run_wide_s, "s", sum_a), (run_wide_d, "d", sum_b), (run_thin[2], "s", sum_c)])
        plan = [(seg1,), (node1,), (seg2,), (node2,), (seg3,), (node3,), (seg4,), (seg5,), (node4,)]

        def paired(eng, total, body):
            body(0, 0, True)
            body(0, 1, True)
            with eng.Fori(1, total // 2) as i:
                body(i, 0, False)
                body(i, 1, False)

        @block.sync
        def _(sp):
            for k, a in (("s", src), ("d", dst)):
                sp.wait_ge(s_key, 2)
                sp.dma_start(keys[k][:, 0:COLS], a[0:P * COLS].rearrange("(p c) -> p c", p=P)).then_inc(s_load, 16)
                sp.dma_start(keys[k][0:REST, COLS:COLS + 1],
                             a[P * COLS:E].rearrange("(p c) -> p c", c=1)).then_inc(s_load, 16)
            sp.wait_ge(s_zero, 1)
            for table in (sorted_s, sorted_d):
                view = table.rearrange("(n p r) w -> n p (r w)", p=P, r=ZR)
                with sp.Fori(0, ROWS // (ZR * P)) as i:
                    sp.dma_start(view[bass.ds(i, 1)].rearrange("a p w -> (a p) w"), zeros[:, :]).then_inc(s_zrow, 16)
            for table in (run_wide_s, run_wide_d, *run_thin):
                w = table.shape[1]
                sp.dma_start(table[0:P, :], zeros[:, 0:w]).then_inc(s_zrow, 16)
            def load(i, s, first):
                if not first:
                    sp.wait_ge(s_pout[s], i * (2 * PB * 16))
                for f, c in ((ef, EF), (et, ET), (stf, STF)):
                    v = f[0:P * COLS].rearrange("(p c) d -> p c d", p=P)
                    sp.dma_start(prow[:, s, :, c:c + D], v[:, bass.ds((2 * i + s) * PB, PB), :]).then_inc(s_pload[s], 16)
            sp.wait_ge(s_const, 1)
            paired(sp, PBATCHES, load)
            sp.wait_ge(s_pout[0], (PBATCHES // 2) * (2 * PB * 16))
            for f, c in ((ef, EF), (et, ET), (stf, STF)):
                sp.dma_start(prow[0:REST, 0, 0, c:c + D], f[P * COLS:E, :]).then_inc(s_rest, 16)

            def seg(q):
                def body(i, s, first):
                    n = 2 * i + s
                    if q.wide:
                        if not first:
                            sp.wait_ge(q.mm, (n - 1) * B)
                            if q is seg1:
                                sp.wait_ge(q.tab[s], 2 * i)
                        sp.dma_start(rows[:, s], q.table_rows.rearrange("(c p) w -> p c w", p=P)[
                            :, bass.ds(n * B, B), :]).then_inc(q.row[s], 16)
                return body

            def store(q):
                def body(i, s, first):
                    n = 2 * i + s
                    sp.wait_ge(q.run, (n + 1) * B)
                    sp.dma_start(q.running.rearrange("(c p) w -> p c w", p=P)[:, bass.ds(n * B + 1, B), :],
                                 run[:, s, :, 0:q.width]).then_inc(q.out[s], 16)
                return body

            for (q,) in plan:
                if isinstance(q, Pass):
                    if q is seg1:
                        for s in range(2):
                            sp.wait_ge(s_pout[s], (PBATCHES // 2) * (2 * PB * 16))
                        sp.wait_ge(s_rout, 32)
                        sp.wait_ge(s_hpad, 1)
                    if q.wide:
                        seg(q)(0, 0, True)
                        seg(q)(0, 1, True)
                    with sp.Fori(1, BATCHES // 2) as i:
                        for s in range(2):
                            store(q)(i - 1, s, False)
                            seg(q)(i, s, False)
                    for s in range(2):
                        store(q)(BATCHES // 2 - 1, s, False)
                elif q is not node4:
                    view = h_dram[q.number].rearrange("(t p) d -> p t d", p=P)
                    with sp.Fori(0, NGROUPS) as i:
                        sp.wait_ge(q.done, i + 1)
                        sp.dma_start(view[:, bass.ds(i * NT, NT), :], h[:, bass.ds(i * NT, NT), :]).then_inc(q.out, 16)
                else:
                    full = out[0:N_FULL * P].rearrange("(t p) d -> p t d", p=P)
                    with sp.Fori(0, NGROUPS - 1) as i:
                        sp.wait_ge(q.done, i + 1)
                        sp.dma_start(full[:, bass.ds(i * NT, NT), :], h[:, bass.ds(i * NT, NT), :]).then_inc(q.out, 16)
                    sp.wait_ge(q.done, NGROUPS)
                    t0 = (NGROUPS - 1) * NT
                    sp.dma_start(full[:, t0:N_FULL, :], h[:, t0:N_FULL, :]).then_inc(q.out, 16)
                    sp.dma_start(out[N_FULL * P:N, :], h[0:N_LAST, N_FULL, :]).then_inc(q.out, 16)
                    sp.wait_ge(q.out, (NGROUPS + 1) * 16)

        @block.gpsimd
        def _(pool):
            pool.iota(iota_tmp[:, 0:P], [[1, P]], base=0, channel_multiplier=0).then_inc(s_iota, 1)
            pool.iota(iota_part_i[:, :], [[0, 1]], base=0, channel_multiplier=1).then_inc(s_iota, 1)
            pool.iota(iota_chunk_i[:, :], [[1, CHUNKS]], base=0, channel_multiplier=0).then_inc(s_iota, 1)
            pool.wait_ge(s_zrow, (2 * (ROWS // (ZR * P)) + 5) * 16)

            def scatter(i, s, first):
                pool.wait_ge(s_pload[s], (i + 1) * 48)
                pool.wait_ge(s_pmeta[s], (i + 1) * 3)
                pool.nop(nofuse=True)
                for j in range(PB):
                    for a, table in ((0, sorted_s), (1, sorted_d)):
                        pool.indirect_dma_start(
                            out=table, out_offset=bass.IndirectOffsetOnAxis(ap=ppos[:, s, a, j:j + 1], axis=0),
                            in_=prow[:, s, j, :], in_offset=None).then_inc(s_pout[s], 16)
            paired(pool, PBATCHES, scatter)
            pool.wait_ge(s_rest, 48)
            pool.wait_ge(s_rmeta, 3)
            pool.nop(nofuse=True)
            for a, table in ((0, sorted_s), (1, sorted_d)):
                pool.indirect_dma_start(
                    out=table, out_offset=bass.IndirectOffsetOnAxis(ap=ppos[0:REST, 0, a, 0:1], axis=0),
                    in_=prow[0:REST, 0, 0, :], in_offset=None).then_inc(s_rout, 16)

            def gather(q):
                def body(i, s, first):
                    n = 2 * i + s
                    if q.wide:
                        pool.wait_ge(q.row[s], (i + 1) * 16)
                    else:
                        pool.wait_ge(q.idx[s], i + 1)
                    if not first:
                        pool.wait_ge(q.mm, (n - 1) * B)
                    pool.nop(nofuse=True)
                    col = ID_D if q.key == "s" else ID_S
                    for b in range(B):
                        ap = rows[:, s, b, col:col + 1].bitcast(I32) if q.wide else gidx[:, s, b:b + 1]
                        pool.indirect_dma_start(
                            out=got[:, s, b, :], out_offset=None, in_=q.table,
                            in_offset=bass.IndirectOffsetOnAxis(ap=ap, axis=0)).then_inc(q.got[s], 16)
                return body

            prev = None
            for (q,) in plan:
                if isinstance(q, Pass):
                    if q is seg5:
                        pool.wait_ge(seg4.mm, CHUNKS)
                    if isinstance(prev, Nodes):
                        pool.wait_ge(prev.out, NGROUPS * 16)
                    paired(pool, BATCHES, gather(q))
                else:
                    segs = {1: [seg1], 2: [seg2], 3: [seg3], 4: [seg1, seg4, seg5]}[q.number]
                    for g in segs:
                        for s in range(2):
                            pool.wait_ge(g.out[s], (BATCHES // 2) * 16)
                    with pool.Fori(0, NGROUPS) as i:
                        pool.wait_ge(q.idx, i + 1)
                        pool.nop(nofuse=True)
                        for a, (running, k, buf) in enumerate(q.sums):
                            for t in range(NT):
                                pool.indirect_dma_start(
                                    out=buf[:, t, :], out_offset=None, in_=running,
                                    in_offset=bass.IndirectOffsetOnAxis(ap=nidx[:, a, t:t + 1], axis=0),
                                ).then_inc(q.sum, 16)
                prev = q

        @block.tensor
        def _(pe):
            pe.wait_ge(s_const, 2)
            for n, k in enumerate("sd"):
                pe.wait_ge(s_oh[k], 1)
                pe.matmul(ps_seg[:, n, 0:LANES * BINS], ones_bf[:, :], onehot[k][:, :, :], start=True,
                          stop=False, skip_group_check=True).then_inc(s_hist[k], 1)
            with pe.Fori(1, STEPS - 1) as j:
                for n, k in enumerate("sd"):
                    pe.wait_ge(s_oh[k], j + 1)
                    pe.matmul(ps_seg[:, n, 0:LANES * BINS], ones_bf[:, :], onehot[k][:, :, :], start=False,
                              stop=False, skip_group_check=True).then_inc(s_hist[k], 1)
            for n, k in enumerate("sd"):
                pe.wait_ge(s_oh[k], STEPS)
                pe.matmul(ps_seg[:, n, 0:LANES * BINS], ones_bf[:, :], onehot[k][:, :, :], start=False,
                          stop=True, skip_group_check=True).then_inc(s_hist[k], 1)
            for n, k in enumerate("sd"):
                pe.wait_ge(s_lane0[k], 1)
                pe.matmul(ps_seg[:, 2 + n, 0:LANES * BINS], ones[0:1, :], lane0[k][0:1, :, :], start=True,
                          stop=False, skip_group_check=True)
            with pe.Fori(0, STEPS) as j:
                for n, k in enumerate("sd"):
                    pe.wait_ge(s_oh[k], j + (STEPS + 1))
                    pe.matmul(ps_seg[:, 2 + n, 0:LANES * BINS], upper[:, :], onehot[k][:, :, :], start=False,
                              stop=False, skip_group_check=True).then_inc(s_rank[k], 1)
                for n, k in enumerate("sd"):
                    pe.wait_ge(s_read[k], j + 1)
                    pe.matmul(ps_seg[:, 2 + n, 0:LANES * BINS], lower[:, :], onehot[k][:, :, :], start=False,
                              stop=False, skip_group_check=True).then_inc(s_hist[k], 1)
            for n, k in enumerate("sd"):
                pe.wait_ge(s_starts, n + 1)
                q4 = CHUNKS // 4
                for a in range(4):
                    mm = pe.matmul(ps_seg[:, a, 0:q4], ones[0:T, :], starts[0:T, a * q4:(a + 1) * q4],
                                   start=True, stop=True)
                mm.then_inc(s_bc, 1)
            pe.wait_ge(s_key, 5)

            def seg(q):
                def body(i, s, first):
                    n = 2 * i + s
                    pe.wait_ge(q.oh[s], i + 1)
                    pe.wait_ge(q.got[s], (i + 1) * (16 * B))
                    for b in range(B):
                        if not (first and s == 0 and b < PS):
                            pe.wait_ge(q.run, n * B + (b - PS + 1))
                        lhs = seg_oh[:, s, b, :]
                        if q.wide:
                            pe.matmul(ps_seg[:, b % PS, 0:FEAT], lhs, rows[:, s, b, 0:FEAT], start=True, stop=True)
                            mm = pe.matmul(ps_seg[:, b % PS, FEAT:WIDE], lhs, got[:, s, b, :], start=True, stop=True)
                        else:
                            mm = pe.matmul(ps_seg[:, b % PS, 0:D], lhs, got[:, s, b, :], start=True, stop=True)
                        mm.then_inc(q.mm, 1)
                return body

            def layer(q):
                w = wts[q.number - 1]
                with pe.Fori(0, NGROUPS) as i:
                    pe.wait_ge(q.cat, i + 1)
                    for t in range(NT):
                        mm = pe.transpose(ps_t[:, t, :], cat[:, t, :], ident[:, :])
                    mm.then_inc(q.tr, 1)
                    pe.wait_ge(q.ct, i + 1)
                    for t in range(NT):
                        mm = pe.matmul(ps_o[:, t, :], catT[:, t, :], w[:, :], start=True, stop=True)
                    mm.then_inc(q.mm, 1)

            def last(q):
                with pe.Fori(0, NGROUPS) as i:
                    pe.wait_ge(q.cat, i * 2 + 1)
                    for t in range(NT):
                        mm = pe.transpose(ps_t[:, t, :], cat[:, t, :], ident[:, :])
                    mm.then_inc(q.tr, 1)
                    pe.wait_ge(q.ct, i * 3 + 1)
                    pe.wait_ge(q.cat2, i + 1)
                    for t in range(NT):
                        mm = pe.transpose(ps_t[:, t, :], cat2[:, t, :], ident[:, :])
                    mm.then_inc(q.tr, 1)
                    pe.wait_ge(q.ct, i * 3 + 2)
                    for t in range(NT):
                        pe.matmul(ps_o[:, t, :], cat2T[:, t, :], w_n2[:, :], start=True, stop=False,
                                  skip_group_check=True)
                        mm = pe.matmul(ps_o[:, t, 0:D], catT[:, t, :], w_n1[:, :], start=False, stop=True,
                                       skip_group_check=True)
                    mm.then_inc(q.mm, 1)
                    pe.wait_ge(q.cat, i * 2 + 2)
                    for t in range(NT):
                        mm = pe.transpose(ps_t[:, t, :], cat[:, t, :], ident[:, :])
                    mm.then_inc(q.tr, 1)
                    pe.wait_ge(q.ct, i * 3 + 3)
                    for t in range(NT):
                        mm = pe.matmul(ps_o[:, t, 0:D], catT[:, t, :], w_n3[:, :], start=True, stop=True)
                    mm.then_inc(q.mm, 1)

            for (q,) in plan:
                if isinstance(q, Pass):
                    if q is seg5:
                        pe.wait_ge(seg4.run, CHUNKS)
                    paired(pe, BATCHES, seg(q))
                elif q is node4:
                    last(q)
                else:
                    if q is node1:
                        pe.wait_ge(s_wload, 16 * 19)
                    layer(q)

        @block.scalar
        def _(act):
            act.wait_ge(s_const, 2)
            for n, (wg, wl, ws, bb) in enumerate(((Wg1, Wl1, Ws1, b1), (Wg2, Wl2, Ws2, b2), (Wgo, Wlo, Wso, bo))):
                act.dma_start(wts[n][0:D, 0:D], wg).then_inc(s_wload, 16)
                act.dma_start(wts[n][0:D, D:P], ws).then_inc(s_wload, 16)
                act.dma_start(wts[n][D:P, D:P], wl).then_inc(s_wload, 16)
                act.dma_start(bias[n][:, :], bb.unsqueeze(0).to_broadcast([P, D])).then_inc(s_wload, 16)
            act.dma_start(w_n1[:, :], W1t[0:2 * D, :]).then_inc(s_wload, 16)
            act.dma_start(w_n2[0:D, 0:D], W1t[2 * D:3 * D, :]).then_inc(s_wload, 16)
            act.dma_start(w_n2[D:P, D:P], W2t[2 * D:3 * D, :]).then_inc(s_wload, 16)
            act.dma_start(w_n3[:, :], W2t[0:2 * D, :]).then_inc(s_wload, 16)
            act.dma_start(bias_n1[:, :], c1.unsqueeze(0).to_broadcast([P, D])).then_inc(s_wload, 16)
            act.dma_start(bias_n2[:, :], c2.unsqueeze(0).to_broadcast([P, D])).then_inc(s_wload, 16)
            act.dma_start(unit[:, :], stf[0:1, :].to_broadcast([P, D])).then_inc(s_wload, 16)
            def place(i, s, first):
                if not first:
                    act.wait_ge(s_pout[s], i * (2 * PB * 16))
                n = 2 * i + s
                act.copy(prow[:, s, :, LOC_S:LOC_S + 4].bitcast(I32), meta[:, bass.ds(n * PB, PB), :]).then_inc(s_pmeta[s], 1)
                for a, k in enumerate("sd"):
                    act.copy(ppos[:, s, a, :], pos[k][:, bass.ds(n * PB, PB)]).then_inc(s_pmeta[s], 1)
            act.wait_ge(s_key, 3)
            paired(act, PBATCHES, place)
            act.wait_ge(s_pout[0], (PBATCHES // 2) * (2 * PB * 16))
            act.copy(prow[0:REST, 0, 0, LOC_S:LOC_S + 4].bitcast(I32), meta[0:REST, COLS, :]).then_inc(s_rmeta, 1)
            for a, k in enumerate("sd"):
                act.copy(ppos[0:REST, 0, a, 0:1], pos[k][0:REST, COLS:COLS + 1]).then_inc(s_rmeta, 1)

            act.wait_ge(s_hpad, 1)
            for buf in (h, xres):
                act.dma_start(buf[:, 0:N_FULL, :], x[0:N_FULL * P].rearrange("(t p) d -> p t d", p=P)).then_inc(s_xload, 16)
                act.dma_start(buf[0:N_LAST, N_FULL, :], x[N_FULL * P:N, :]).then_inc(s_xload, 16)

            def keep_idx(q):
                def body(i, s, first):
                    n = 2 * i + s
                    act.wait_ge(q.row[s], (i + 1) * 16)
                    act.copy(loc_s[:, bass.ds(n * B, B)], rows[:, s, :, LOC_S].bitcast(I32)).then_inc(q.tab[s], 1)
                    act.copy(id_d[:, bass.ds(n * B, B)], rows[:, s, :, ID_D].bitcast(I32)).then_inc(q.tab[s], 1)
                return body

            def place_idx(q):
                def body(i, s, first):
                    n = 2 * i + s
                    if not first:
                        act.wait_ge(q.got[s], i * (16 * B))
                    act.copy(gidx[:, s, :], id_d[:, bass.ds(n * B, B)]).then_inc(q.idx[s], 1)
                return body

            for (q,) in plan:
                if isinstance(q, Pass):
                    if q is seg1:
                        paired(act, BATCHES, keep_idx(q))
                        for s in range(2):
                            act.wait_ge(q.tab[s], BATCHES)
                    elif not q.wide:
                        paired(act, BATCHES, place_idx(q))
                    continue
                copies = 3 if q is node4 else 1

                def group(i, first):
                    if not first:
                        act.wait_ge(q.sum, i * (16 * NT * len(q.sums)))
                    for a, (running, k, buf) in enumerate(q.sums):
                        ins = act.copy(nidx[:, a, :], lastrow[k][:, bass.ds(i * NT, NT)])
                    ins.then_inc(q.idx, 1)
                    for c in range(copies):
                        act.wait_ge(q.tr, i * copies + (c + 1))
                        to = cat2T if c == 1 else catT
                        act.copy(to[:, 0:4, :], ps_t[:, 0:4, :])
                        act.copy(to[:, 4:NT, :], ps_t[:, 4:NT, :]).then_inc(q.ct, 1)
                    if q is not node4:
                        act.wait_ge(q.neg, i + 1)
                        act.activation(nb[:, :, :], nb[:, :, :], ACT.Exp).then_inc(q.exp, 1)
                    if q in (node3, node4):
                        act.wait_ge(q.var, i + 1)
                        act.activation(nm[:, :, 2], nm[:, :, 1], ACT.Sqrt).then_inc(q.std, 1)
                group(0, True)
                with act.Fori(1, NGROUPS) as i:
                    group(i, False)

        @block.vector
        def _(dve):
            dve.memset(zeros[:, :], 0.0).then_inc(s_zero, 1)
            for k in "sd":
                dve.memset(keys[k][:, COLS:KEYC], T * P).then_inc(s_key, 1)
            dve.wait_ge(s_key, 2)
            dve.memset(prow[:, :, :, ONE:ONE + 1], 1.0)
            dve.memset(prow[:, :, :, ID_S + 1:ROW], 0.0).then_inc(s_const, 1)
            dve.memset(ones_bf[:, :], 1.0)
            dve.memset(ones[:, :], 1.0)
            for wmat in (*wts, w_n2):
                dve.memset(wmat[:, :], 0.0)
            dve.wait_ge(s_iota, 3)
            dve.tensor_copy(iota_part[:, :], iota_part_i[:, :])
            chain(dve, dve.tensor_copy(iota_row[:, :], iota_tmp[:, :]))
            dve.tensor_copy(iota_bin[:, :], iota_tmp[:, 0:BINS])
            dve.tensor_scalar(iota_loc[:, :], iota_row[:, :], 1.0, None, ALU.add)
            dve.tensor_scalar(ident[:, :], iota_row[:, :], iota_part[:, 0:1], None, ALU.is_equal)
            dve.tensor_scalar(upper[:, :], iota_row[:, :], iota_part[:, 0:1], None, ALU.is_gt)
            dve.tensor_scalar(lower[:, :], iota_row[:, :], iota_part[:, 0:1], None, ALU.is_le).then_inc(s_const, 1)
            dve.wait_ge(s_const, 2)

            dve.wait_ge(s_load, 64)
            for n, (k, other) in enumerate((("s", "d"), ("d", "s"))):
                chain(dve, dve.tensor_scalar(meta[:, :, 0], keys[k][:, :], 7, None, ALU.logical_shift_right))
                chain(dve, dve.tensor_copy(tid[k][:, :], meta[:, :, 0]))
            for n, (k, other) in enumerate((("s", "d"), ("d", "s"))):
                chain(dve, dve.tensor_scalar(meta[:, :, 2 * n], keys[k][:, :], P - 1, None, ALU.bitwise_and))
                chain(dve, dve.tensor_scalar(meta[:, :, 2 * n], meta[:, :, 2 * n], 1.0, None, ALU.add))
                chain(dve, dve.tensor_copy(meta[:, :, 2 * n + 1], keys[other][:, :]))

            def bins_of(k, j):
                return dve.tensor_tensor(
                    onehot[k][:, :, :], tid[k][:, bass.ds(j * LANES, LANES)].unsqueeze(2).to_broadcast([P, LANES, BINS]),
                    iota_bin[:, :].unsqueeze(1).to_broadcast([P, LANES, BINS]), ALU.is_equal)

            for k in "sd":
                bins_of(k, 0).then_inc(s_oh[k], 1)
            with dve.Fori(1, STEPS) as j:
                for k in "sd":
                    dve.wait_ge(s_hist[k], j)
                    bins_of(k, j).then_inc(s_oh[k], 1)
            for n, k in enumerate("sd"):
                dve.wait_ge(s_hist[k], STEPS)
                chain(dve, dve.tensor_copy(prod[k][:, :, :], ps_seg[:, n, 0:LANES * BINS].rearrange(
                    "p (l b) -> p l b", l=LANES)))
                chain(dve, dve.tensor_reduce(count[k][:, :], prod[k][:, :, :].rearrange("p l b -> p b l"), AX.X, ALU.add))
                chain(dve, dve.tensor_scalar(nchunk_i[k][:, :], count[k][:, :], float(P - 1), None, ALU.add))
                chain(dve, dve.tensor_scalar(nchunk_i[k][:, :], nchunk_i[k][:, :], 7, None, ALU.logical_shift_right))
                chain(dve, dve.tensor_copy(nchunk[k][:, :], nchunk_i[k][:, :]))
                chain(dve, dve.tensor_tensor_scan(cend[k][:, :], nchunk[k][:, :], nchunk[k][:, :], 0.0, ALU.add, ALU.bypass))
                chain(dve, dve.tensor_tensor(cstart[k][:, :], cend[k][:, :], nchunk[k][:, :], ALU.subtract))
                chain(dve, dve.tensor_scalar(filled[k][:, :], nchunk[k][:, :], 1.0, None, ALU.min))
                chain(dve, dve.tensor_scalar(lane0[k][:, 0, :], cstart[k][:, :], float(P), None, ALU.mult))
                for l in range(1, LANES):
                    ins = dve.tensor_tensor(lane0[k][:, l, :], lane0[k][:, l - 1, :], prod[k][:, l - 1, :], ALU.add)
                    if l < LANES - 1:
                        chain(dve, ins)
                ins.then_inc(s_lane0[k], 1)

            def rank(j, first):
                for k in "sd":
                    if first:
                        dve.wait_ge(s_hist[k], STEPS)
                    else:
                        dve.wait_ge(s_hist[k], j + STEPS)
                    bins_of(k, j).then_inc(s_oh[k], 1)
                for n, k in enumerate("sd"):
                    dve.wait_ge(s_rank[k], j + 1)
                    dve.tensor_tensor(prod[k][:, :, :], onehot[k][:, :, :],
                                      ps_seg[:, 2 + n, 0:LANES * BINS].rearrange("p (l b) -> p l b", l=LANES),
                                      ALU.mult).then_inc(s_read[k], 1)
                    dve.wait_ge(s_read[k], j + 1)
                    dve.tensor_reduce(pos[k][:, bass.ds(j * LANES, LANES)], prod[k][:, :, :], AX.X,
                                      ALU.add).then_inc(s_prod[k], 1)
                    dve.wait_ge(s_prod[k], j + 1)
            rank(0, True)
            with dve.Fori(1, STEPS) as j:
                rank(j, False)
            for k in "sd":
                dve.wait_ge(s_hist[k], 2 * STEPS)
            dve.memset(binsq[:, :], 0.0).then_inc(s_key, 1)
            dve.wait_ge(s_key, 3)

            for n, k in enumerate("sd"):
                for row, col in ((cstart, startcol), (filled, fillcol)):
                    chain(dve, dve.tensor_tensor(binsq[:, :], row[k][:, :], ident[:, 0:BINS], ALU.mult))
                    chain(dve, dve.tensor_reduce(col[k][:, :], binsq[:, :], AX.X, ALU.add))
                if n == 1:
                    dve.wait_ge(s_bc, 1)
                dve.tensor_scalar(starts[:, :], iota_chunk_i[:, :], startcol[k][:, 0:1], fillcol[k][:, 0:1],
                                  ALU.is_equal, ALU.mult).then_inc(s_starts, 1)
                dve.wait_ge(s_bc, n + 1)
                q4 = CHUNKS // 4
                dve.tensor_scalar(keep[k][:, :].rearrange("p (a c) -> p a c", a=4), ps_seg[:, :, 0:q4],
                                  -1.0, 1.0, ALU.mult, ALU.add).then_inc(s_key, 1)
                chain(dve, dve.tensor_tensor(binsq[:, :], cend[k][:, :], filled[k][:, :], ALU.mult))
                chain(dve, dve.tensor_scalar(lastrow[k][:, :], binsq[:, 0:T], float(P), iota_part[:, 0:1],
                                             ALU.mult, ALU.add))
            dve.wait_ge(s_key, 5)

            for s in range(2):
                dve.wait_ge(s_pout[s], (PBATCHES // 2) * (2 * PB * 16))
            dve.wait_ge(s_rout, 32)
            dve.memset(loc_s[:, CHUNKS:CHUNKS + B], 0)
            dve.memset(xres[:, N_FULL, :], 0.0)
            dve.memset(h[:, N_FULL, :], 0.0)
            chain(dve, dve.memset(run[:, :, :, :], 0.0))
            dve.memset(nm[:, :, :], 0.0).then_inc(s_hpad, 1)

            def onehots(q, i, s, first):
                n = 2 * i + s
                if not first:
                    dve.wait_ge(q.mm, (n - 1) * B)
                if q.wide:
                    dve.wait_ge(q.row[s], (i + 1) * 16)
                    col = LOC_S if q.key == "s" else LOC_D
                    loc = rows[:, s, :, col:col + 1].bitcast(I32)
                else:
                    loc = loc_s[:, bass.ds(n * B, B)].unsqueeze(2)
                dve.tensor_tensor(seg_oh[:, s], loc.to_broadcast([P, B, P]),
                                  iota_loc[:, :].unsqueeze(1).to_broadcast([P, B, P]),
                                  ALU.is_equal).then_inc(q.oh[s], 1)

            def running(q, i, s, first):
                n = 2 * i + s
                w = q.width
                if not first:
                    dve.wait_ge(q.out[s], i * 16)
                for b in range(B):
                    dve.wait_ge(q.mm, n * B + (b + 1))
                    if not (first and s == 0 and b == 0):
                        dve.wait_ge(q.run, n * B + b)
                    before = run[:, s, b - 1, 0:w] if b else run[:, 1 - s, B - 1, 0:w]
                    dve.scalar_tensor_tensor(
                        run[:, s, b, 0:w], before, keep[q.key][:, bass.ds(n * B + b, 1)],
                        ps_seg[:, b % PS, 0:w], ALU.mult, ALU.add).then_inc(q.run, 1)

            def seg(q):
                onehots(q, 0, 0, True)
                onehots(q, 0, 1, True)
                running(q, 0, 0, True)
                onehots(q, 1, 0, False)
                running(q, 0, 1, True)
                with dve.Fori(1, BATCHES // 2 - 1) as i:
                    onehots(q, i, 1, False)
                    running(q, i, 0, False)
                    onehots(q, i + 1, 0, False)
                    running(q, i, 1, False)
                i = BATCHES // 2 - 1
                onehots(q, i, 1, False)
                running(q, i, 0, False)
                running(q, i, 1, False)

            def bc(ap):
                return ap.unsqueeze(2).to_broadcast([P, NT, D])

            class Steps:

                def __init__(self, q, i, per):
                    self.q, self.i, self.per, self.n = q, i, per, 0

                def __call__(self, ins):
                    self.n += 1
                    ins.then_inc(self.q.v, 1)
                    dve.wait_ge(self.q.v, self.i * self.per + self.n)

            def layernorm(q, step, i):
                hs = h[:, bass.ds(i * NT, NT), :]
                step(dve.tensor_reduce(nm[:, :, 0], na[:, :, :], AX.X, ALU.add))
                step(dve.tensor_scalar(nm[:, :, 0], nm[:, :, 0], 1.0 / D, None, ALU.mult))
                step(dve.tensor_tensor(na[:, :, :], na[:, :, :], bc(nm[:, :, 0]), ALU.subtract))
                step(dve.tensor_tensor(nb[:, :, :], na[:, :, :], na[:, :, :], ALU.mult))
                step(dve.tensor_reduce(nm[:, :, 1], nb[:, :, :], AX.X, ALU.add))
                dve.tensor_scalar(nm[:, :, 1], nm[:, :, 1], 1.0 / D, EPS, ALU.mult, ALU.add).then_inc(q.var, 1)
                dve.wait_ge(q.std, i + 1)
                step(dve.reciprocal(nm[:, :, 3], nm[:, :, 2]))
                dve.tensor_tensor(hs, na[:, :, :], bc(nm[:, :, 3]), ALU.mult).then_inc(q.done, 1)
                dve.wait_ge(q.done, i + 1)

            def layer(q):
                wide = q is node1
                normed = q is node3
                per = (4 if wide else 0) + 5 + (8 if normed else 0)
                with dve.Fori(0, NGROUPS) as i:
                    step = Steps(q, i, per)
                    ts = bass.ds(i * NT, NT)
                    hs = h[:, ts, :]
                    dve.wait_ge(q.sum, (i + 1) * (16 * NT))
                    if wide:
                        step(dve.tensor_scalar(linked[:, ts], sum_a[:, :, ONE], 1.0, None, ALU.min))
                        step(dve.tensor_scalar(nm[:, :, 4], sum_a[:, :, ONE], 1.0, None, ALU.max))
                        step(dve.reciprocal(nm[:, :, 5], nm[:, :, 4]))
                        step(dve.tensor_scalar(inv[:, ts], nm[:, :, 5], 1.0, None, ALU.mult))
                        agg = sum_a[:, :, FEAT:WIDE]
                    else:
                        agg = sum_c[:, :, :]
                    step(dve.tensor_scalar(cat[:, :, 0:D], hs, 1.0, None, ALU.mult))
                    dve.tensor_tensor(cat[:, :, D:P], agg, bc(inv[:, ts]), ALU.mult).then_inc(q.cat, 1)
                    dve.wait_ge(q.mm, i + 1)
                    step(dve.tensor_tensor(na[:, :, :], ps_o[:, 0:NT, 0:D],
                                           bias[q.number - 1][:, :].unsqueeze(1).to_broadcast([P, NT, D]), ALU.add))
                    step(dve.tensor_tensor(nb[:, :, :], ps_o[:, 0:NT, D:P], bc(linked[:, ts]), ALU.mult))
                    step(dve.tensor_tensor(na[:, :, :], na[:, :, :], nb[:, :, :], ALU.add))
                    dve.tensor_scalar(nb[:, :, :], na[:, :, :], 0.0, None, ALU.min).then_inc(q.neg, 1)
                    step(dve.tensor_scalar(cat[:, :, 0:D], na[:, :, :], 0.0, -1.0, ALU.max, ALU.add))
                    dve.wait_ge(q.exp, i + 1)
                    if not normed:
                        dve.tensor_tensor(hs, cat[:, :, 0:D], nb[:, :, :], ALU.add).then_inc(q.done, 1)
                        dve.wait_ge(q.done, i + 1)
                    else:
                        step(dve.tensor_tensor(na[:, :, :], cat[:, :, 0:D], nb[:, :, :], ALU.add))
                        step(dve.tensor_tensor(na[:, :, :], na[:, :, :], xres[:, ts, :], ALU.add))
                        layernorm(q, step, i)
                    assert step.n == per, step.n

            def last(q):
                with dve.Fori(0, NGROUPS) as i:
                    step = Steps(q, i, 19)
                    ts = bass.ds(i * NT, NT)
                    hs = h[:, ts, :]
                    dve.wait_ge(q.sum, (i + 1) * (16 * NT * 3))
                    u = unit[:, :].unsqueeze(1).to_broadcast([P, NT, D])
                    step(dve.tensor_tensor(na[:, :, :], sum_c[:, :, :], sum_b[:, :, FEAT:WIDE], ALU.add))
                    step(dve.tensor_tensor(cat[:, :, 0:D], na[:, :, :], hs, ALU.add))
                    step(dve.tensor_tensor(sum_a[:, :, 0:FEAT], sum_a[:, :, 0:FEAT], sum_b[:, :, 0:FEAT], ALU.add))
                    dve.tensor_copy(cat[:, :, D:P], sum_a[:, :, EF:EF + D]).then_inc(q.cat, 1)
                    step(dve.tensor_scalar(nm[:, :, 4], sum_a[:, :, ONE], 1.0, None, ALU.add))
                    step(dve.reciprocal(nm[:, :, 5], nm[:, :, 4]))
                    step(dve.tensor_tensor(cat2[:, :, 0:D], sum_a[:, :, ET:ET + D], u, ALU.add))
                    step(dve.tensor_tensor(nb[:, :, :], sum_a[:, :, STF:STF + D], u, ALU.add))
                    dve.tensor_tensor(cat2[:, :, D:P], nb[:, :, :], bc(nm[:, :, 5]), ALU.mult).then_inc(q.cat2, 1)
                    dve.wait_ge(q.cat2, i + 1)
                    step(dve.tensor_tensor(nb[:, :, :], bias_n1[:, :].unsqueeze(1).to_broadcast([P, NT, D]),
                                           bc(nm[:, :, 4]), ALU.mult))
                    dve.wait_ge(q.mm, i * 2 + 1)
                    step(dve.tensor_tensor(na[:, :, :], ps_o[:, 0:NT, 0:D], nb[:, :, :], ALU.add))
                    step(dve.tensor_scalar(cat[:, :, D:P], hs, 1.0, None, ALU.mult))
                    dve.tensor_scalar(cat[:, :, 0:D], na[:, :, :], 0.0, None, ALU.max).then_inc(q.cat, 1)
                    dve.wait_ge(q.mm, i * 2 + 2)
                    step(dve.tensor_tensor(na[:, :, :], ps_o[:, 0:NT, 0:D],
                                           bias_n2[:, :].unsqueeze(1).to_broadcast([P, NT, D]), ALU.add))
                    step(dve.tensor_tensor(na[:, :, :], na[:, :, :], ps_o[:, 0:NT, D:P], ALU.add))
                    step(dve.tensor_tensor(na[:, :, :], na[:, :, :], hs, ALU.add))
                    layernorm(q, step, i)
                    assert step.n == 19, step.n

            for (q,) in plan:
                if isinstance(q, Pass):
                    if q is seg2:
                        for s in range(2):
                            dve.wait_ge(seg1.tab[s], BATCHES)
                    if q is seg5:
                        for s in range(2):
                            dve.wait_ge(seg4.out[s], (BATCHES // 2) * 16)
                    seg(q)
                elif q is node4:
                    last(q)
                else:
                    if q is node1:
                        dve.wait_ge(s_wload, 16 * 19)
                        dve.wait_ge(s_xload, 64)
                    layer(q)


_INS = ["x", "src", "dst", "edge_attr_64", "edge_attr_64_n2", "edge_attr_64_n3",
        "L0_gnn_Wg1", "L0_gnn_Wl1", "L0_gnn_Ws1", "L0_gnn_b1", "L0_gnn_Wg2", "L0_gnn_Wl2", "L0_gnn_Ws2", "L0_gnn_b2",
        "L0_gnn_Wgo", "L0_gnn_Wlo", "L0_gnn_Wso", "L0_gnn_bo", "L1_gnn_W1", "L1_gnn_b1", "L1_gnn_W2", "L1_gnn_b2"]


def kernel(**inputs):
    import concourse.bacc as bacc
    from concourse.bass_utils import run_bass_kernel_spmd

    nc = bacc.Bacc("TRN2", target_bir_lowering=False, num_devices=1)
    arrays, args = {}, []
    for name in _INS:
        a = np.asarray(inputs[name])
        if name in ("L1_gnn_W1", "L1_gnn_W2"):
            a = a.T
        a = np.ascontiguousarray(a)
        arrays[f"in_{name}"] = a
        args.append(nc.dram_tensor(f"in_{name}", a.shape, mybir.dt.from_np(a.dtype), kind="ExternalInput").ap())
    args.append(nc.dram_tensor("out_x", (N, D), F32, kind="ExternalOutput").ap())
    build(nc, *args)
    r = run_bass_kernel_spmd(nc, [arrays], core_ids=[0])
    return r.results[0]["out_x"]
```

```python
from contextlib import ExitStack

import numpy as np

import concourse.bass as bass
from concourse import mybir

ALU = mybir.AluOpType
ACT = mybir.ActivationFunctionType
AX = mybir.AxisListType
F32 = mybir.dt.float32
BF16 = mybir.dt.bfloat16
I32 = mybir.dt.int32

P = 128
D = 64
N = 12500
E = 200000
T = -(-N // P)
N_FULL = N // P
N_LAST = N - N_FULL * P
EPS = 1e-5

COLS = E // P
REST = E - COLS * P
LANES = 5
STEPS = -(-(COLS + 1) // LANES)
KEYC = STEPS * LANES
BINS = T + 1

B = 4
SLOTS = 4
CHUNKS = -(-(E // P + T + 1) // (SLOTS * B)) * (SLOTS * B)
BATCHES = CHUNKS // B
ROWS = CHUNKS * P

EF, ET, STF, ONE, LOC, OTHER, ROW = 0, D, 2 * D, 3 * D, 3 * D + 1, 3 * D + 2, 3 * D + 4
FEAT = ONE + 1
WIDE = FEAT + D

PB = 11
PBATCHES = COLS // PB
ZR = 8
NT = 7
NGROUPS = T // NT
MARKS = CHUNKS // 4

BESIDE = {1: (2, 4), 2: (2 + 4 * NGROUPS, 4), 3: (2 + 8 * NGROUPS, 2)}

assert COLS % (2 * PB) == 0 and ROWS % (ZR * P) == 0 and T % NT == 0 and NGROUPS % 2 == 0
assert 2 + 10 * NGROUPS == PBATCHES


def is_first(i):
    return isinstance(i, int) and i == 0


def build(nc, x, src, dst, ef, stf, et, Wg1, Wl1, Ws1, b1, Wg2, Wl2, Ws2, b2, Wgo, Wlo, Wso, bo,
          W1t, c1, W2t, c2, out):
    with ExitStack() as ctx:
        early = ExitStack()

        def sb(name, shape, dt=F32):
            return ctx.enter_context(nc.sbuf_tensor(name, shape, dt))

        def sb_early(name, shape, dt=F32):
            return early.enter_context(nc.sbuf_tensor(name, shape, dt))

        def sem(name):
            return ctx.enter_context(nc.semaphore(name))

        def dram(name, shape):
            return nc.dram_tensor(name, shape, F32).ap()

        sorted_s = dram("sorted_by_src", (ROWS, ROW))
        sorted_d = dram("sorted_by_dst", (ROWS, ROW))
        h_dram = [None, dram("h1", (T * P, D)), dram("h2", (T * P, D)), dram("x1", (T * P, D))]
        run_wide_s = dram("run_wide_s", ((CHUNKS + 1) * P, WIDE))
        run_wide_d = dram("run_wide_d", ((CHUNKS + 1) * P, WIDE))
        run_thin = [dram(f"run_thin{i}", ((CHUNKS + 1) * P, D)) for i in range(3)]

        ps_seg = ctx.enter_context(nc.psum_tensor("ps_seg", [P, B, 512], F32))
        ps_t = ctx.enter_context(nc.psum_tensor("ps_t", [P, 8, P], F32))
        ps_o = ctx.enter_context(nc.psum_tensor("ps_o", [P, 8, P], F32))

        iota_bin = sb("iota_bin", [P, BINS], BF16)
        iota_loc = sb("iota_loc", [P, P], BF16)
        iota_row = sb("iota_row", [P, P])
        iota_part = sb("iota_part", [P, 1])
        iota_part_i = sb("iota_part_i", [P, 1], I32)
        upper = sb("upper", [P, P], BF16)
        lower = sb("lower", [P, P], BF16)
        ones_bf = sb("ones_bf", [P, P], BF16)
        ones = sb("ones", [P, P])
        ident = sb("ident", [P, P])
        keep = {k: sb(f"keep_{k}", [P, CHUNKS], BF16) for k in "sd"}
        lastrow = {k: sb(f"lastrow_{k}", [P, T], I32) for k in "sd"}

        wts = [sb(f"wts{i}", [P, P]) for i in range(3)]
        bias = [sb(f"bias{i}", [P, D]) for i in range(3)]
        w_n1 = sb("w_n1", [P, D])
        w_n2 = sb("w_n2", [P, P])
        w_n3 = sb("w_n3", [P, D])
        bias_n1 = sb("bias_n1", [P, D])
        bias_n2 = sb("bias_n2", [P, D])
        unit = sb("unit", [P, D])

        keys = {k: sb(f"keys_{k}", [P, KEYC], I32) for k in "sd"}
        place = {k: sb(f"place_{k}", [P, KEYC], BF16) for k in "sd"}
        pos = {k: sb(f"pos_{k}", [P, KEYC]) for k in "sd"}
        prow = sb("prow", [P, 2, PB, ROW])
        ppos = sb("ppos", [P, 2, PB], I32)

        rows = sb("rows", [P, SLOTS, B, ROW])
        seg_oh = sb("seg_oh", [P, SLOTS, B, P])
        got = sb("got", [P, SLOTS, B, D])
        gidx = sb("gidx", [P, SLOTS, B], I32)
        loc_s = sb("loc_s", [P, CHUNKS + B], BF16)
        id_d = sb("id_d", [P, CHUNKS], I32)
        run = sb("run", [P, 2, 2 * B, WIDE])

        inv = sb("inv", [P, T])
        linked = sb("linked", [P, T])
        nidx = sb("nidx", [P, 2, 3, NT], I32)
        sum_a = sb("sum_a", [P, NT, WIDE])
        sum_b = sb("sum_b", [P, NT, WIDE])
        sum_c = sb("sum_c", [P, NT, D])
        flat = run[:, :, :, :].rearrange("p a b w -> p (a b w)")
        spare_a = flat[:, 0:NT * WIDE].rearrange("p (t w) -> p t w", w=WIDE)
        spare_b = flat[:, NT * WIDE:2 * NT * WIDE].rearrange("p (t w) -> p t w", w=WIDE)
        spare_c = flat[:, 2 * NT * WIDE:2 * NT * WIDE + NT * D].rearrange("p (t w) -> p t w", w=D)
        cat = sb("cat", [P, NT, P])
        cat2 = sb("cat2", [P, NT, P])
        catT = sb("catT", [P, NT, P])
        cat2T = sb("cat2T", [P, NT, P])
        na = sb("na", [P, NT, D])
        nb = sb("nb", [P, NT, D])
        nm = sb("nm", [P, NT, 8])
        xres = sb("xres", [P, NT, D])

        iota_tmp = sb_early("iota_tmp", [P, P], I32)
        iota_mark = sb_early("iota_mark", [P, MARKS], I32)
        zeros = sb_early("zeros", [P, ZR * ROW])
        bits = sb_early("bits", [P, KEYC], I32)
        tid = sb_early("tid", [P, KEYC], BF16)
        onehot = sb_early("onehot", [P, 2, LANES, BINS], BF16)
        prod = sb_early("prod", [P, LANES, BINS])
        lane0 = sb_early("lane0", [P, LANES, BINS])
        count, nchunk, cend, cstart, filled, binsq = (
            sb_early(n, [P, BINS]) for n in ("count", "nchunk", "cend", "cstart", "filled", "binsq"))
        nchunk_i = sb_early("nchunk_i", [P, BINS], I32)
        startcol = sb_early("startcol", [P, 1])
        fillcol = sb_early("fillcol", [P, 1])
        starts = sb_early("starts", [P, 4, MARKS])
        early.close()
        h = sb("h", [P, T, D])

        s_const = sem("s_const")
        s_iota = sem("s_iota")
        s_load = {k: sem(f"s_load_{k}") for k in "sd"}
        s_wload = sem("s_wload")
        s_xload = sem("s_xload")
        s_hpad = sem("s_hpad")
        s_zero = sem("s_zero")
        s_zrow = {k: sem(f"s_zrow_{k}") for k in "sd"}
        s_pad = sem("s_pad")
        s_v = sem("s_v")
        s_oh = sem("s_oh")
        s_mul = sem("s_mul")
        s_lane0 = sem("s_lane0")
        s_rank = sem("s_rank")
        s_read = sem("s_read")
        s_prod = sem("s_prod")
        s_ranked = sem("s_ranked")
        s_starts = sem("s_starts")
        s_bc = sem("s_bc")
        s_keep = sem("s_keep")

        vcount = [0]

        def chain(dve, ins):
            vcount[0] += 1
            ins.then_inc(s_v, 1)
            dve.wait_ge(s_v, vcount[0])

        block = ctx.enter_context(nc.Block())

        class Sort:

            def __init__(self, name, key, other, table):
                self.key, self.other, self.table = key, other, table
                self.load = [sem(f"{name}_load{i}") for i in range(2)]
                self.meta = [sem(f"{name}_meta{i}") for i in range(2)]
                self.out = [sem(f"{name}_out{i}") for i in range(2)]
                self.rest_load, self.rest_meta, self.rest_out = (sem(f"{name}_rest{i}") for i in range(3))

        sort_s = Sort("sort_s", "s", "d", sorted_s)
        sort_d = Sort("sort_d", "d", "s", sorted_d)
        SORTED = (PBATCHES // 2) * (PB * 16)

        class Pass:

            def __init__(self, name, key, table, running, table_rows):
                self.key, self.table, self.running, self.table_rows = key, table, running, table_rows
                self.wide = table_rows is not None
                self.width = WIDE if self.wide else D
                if self.wide:
                    self.row = [sem(f"{name}_row{i}") for i in range(SLOTS)]
                else:
                    self.idx = sem(f"{name}_idx")
                if name == "seg1":
                    self.tab = sem(f"{name}_tab")
                self.got = [sem(f"{name}_got{i}") for i in range(SLOTS)]
                self.oh = sem(f"{name}_oh")
                self.mm = sem(f"{name}_mm")
                self.run = sem(f"{name}_run")
                self.out = [sem(f"{name}_out{i}") for i in range(2)]

        HALVES = BATCHES // 4

        seg1 = Pass("seg1", "s", x, run_wide_s, sorted_s)
        seg2 = Pass("seg2", "s", h_dram[1], run_thin[0], None)
        seg3 = Pass("seg3", "s", h_dram[2], run_thin[1], None)
        seg4 = Pass("seg4", "s", h_dram[3], run_thin[2], None)
        seg5 = Pass("seg5", "d", h_dram[3], run_wide_d, sorted_d)

        class Nodes:

            def __init__(self, name, number, sums):
                self.number, self.sums = number, sums
                self.idx = sem(f"{name}_idx")
                self.sum = [sem(f"{name}_sum{i}") for i in range(2 if number == 4 else 1)]
                self.cat = sem(f"{name}_cat")
                self.tr = sem(f"{name}_tr")
                self.ct = sem(f"{name}_ct")
                self.mm = sem(f"{name}_mm")
                if number == 4:
                    self.cat2 = sem(f"{name}_cat2")
                else:
                    self.neg = sem(f"{name}_neg")
                    self.exp = sem(f"{name}_exp")
                if number >= 3:
                    self.var = sem(f"{name}_var")
                    self.std = sem(f"{name}_std")
                self.v = sem(f"{name}_v")
                self.done = sem(f"{name}_done")
                self.out = sem(f"{name}_out")

        node1 = Nodes("node1", 1, [(run_wide_s, "s", [sum_a])])
        node2 = Nodes("node2", 2, [(run_thin[0], "s", [sum_c])])
        node3 = Nodes("node3", 3, [(run_thin[1], "s", [sum_c])])
        node4 = Nodes("node4", 4, [(run_wide_s, "s", [sum_a, spare_a]), (run_wide_d, "d", [sum_b, spare_b]),
                                   (run_thin[2], "s", [sum_c, spare_c])])
        plan = [seg1, node1, seg2, node2, seg3, node3, seg4, seg5, node4]

        def batches(eng, body):
            for s in range(SLOTS):
                body(0, s, True)
            with eng.Fori(1, BATCHES // SLOTS) as i:
                for s in range(SLOTS):
                    body(i, s, False)

        def sort_batches(eng, q, body):
            for s in range(2):
                body(q, s, 0)
            with eng.Fori(1, PBATCHES // 2) as i:
                for s in range(2):
                    body(q, s, i)

        def beside(q, i, js, body):
            base, per = BESIDE[q.number]
            for j in js:
                if j < per:
                    body(sort_d, j % 2, i * (per // 2) + (base // 2 + j // 2))

        @block.sync
        def _(sp):
            for k, a in (("s", src), ("d", dst)):
                sp.wait_ge(s_pad, 2)
                sp.dma_start(keys[k][:, 0:COLS], a[0:P * COLS].rearrange("(p c) -> p c", p=P)).then_inc(s_load[k], 16)
                sp.dma_start(keys[k][0:REST, COLS:COLS + 1],
                             a[P * COLS:E].rearrange("(p c) -> p c", c=1)).then_inc(s_load[k], 16)
            sp.wait_ge(s_zero, 1)
            for k, table in (("s", sorted_s), ("d", sorted_d)):
                view = table.rearrange("(n p r) w -> n p (r w)", p=P, r=ZR)
                with sp.Fori(0, ROWS // (ZR * P)) as i:
                    sp.dma_start(view[bass.ds(i, 1)].rearrange("a p w -> (a p) w"), zeros[:, :]).then_inc(s_zrow[k], 16)
                if k == "s":
                    for running in (run_wide_s, run_wide_d, *run_thin):
                        w = running.shape[1]
                        sp.dma_start(running[0:P, :], zeros[:, 0:w]).then_inc(s_zrow[k], 16)

            def load(q, s, use):
                if not is_first(use):
                    sp.wait_ge(q.out[s], use * (PB * 16))
                elif q is sort_d:
                    sp.wait_ge(sort_s.out[s], SORTED)
                    if s == 0:
                        sp.wait_ge(sort_s.rest_out, 16)
                sp.nop(nofuse=True)
                for f, c in ((ef, EF), (et, ET), (stf, STF)):
                    v = f[0:P * COLS].rearrange("(p c) d -> p c d", p=P)
                    sp.dma_start(prow[:, s, :, c:c + D], v[:, bass.ds((2 * use + s) * PB, PB), :]).then_inc(q.load[s], 16)

            def load_rest(q):
                sp.wait_ge(q.out[0], SORTED)
                for f, c in ((ef, EF), (et, ET), (stf, STF)):
                    sp.dma_start(prow[0:REST, 0, 0, c:c + D], f[P * COLS:E, :]).then_inc(q.rest_load, 16)

            sort_batches(sp, sort_s, load)
            load_rest(sort_s)

            def fetch(q):
                def body(i, s, first):
                    n = SLOTS * i + s
                    if not first:
                        sp.wait_ge(q.mm, (n - SLOTS + 1) * B)
                        sp.nop(nofuse=True)
                        if q is seg1:
                            sp.wait_ge(q.tab, 2 * (n - SLOTS + 1))
                    sp.nop(nofuse=True)
                    sp.dma_start(rows[:, s], q.table_rows.rearrange("(c p) w -> p c w", p=P)[
                        :, bass.ds(n * B, B), :]).then_inc(q.row[s], 16)
                return body

            def store(q, i, half):
                n = SLOTS * i + 2 * half
                sp.wait_ge(q.run, (n + 2) * B)
                sp.nop(nofuse=True)
                sp.dma_start(q.running.rearrange("(c p) w -> p c w", p=P)[:, bass.ds(n * B + 1, 2 * B), :],
                             run[:, half, :, 0:q.width]).then_inc(q.out[half], 16)

            for q in plan:
                if isinstance(q, Pass):
                    if q is seg1:
                        for s in range(2):
                            sp.wait_ge(sort_s.out[s], SORTED)
                        sp.wait_ge(sort_s.rest_out, 16)
                        for s in range(SLOTS):
                            fetch(seg1)(0, s, True)
                    if q is seg4:
                        load_rest(sort_d)
                        for s in range(2):
                            sp.wait_ge(sort_d.out[s], SORTED)
                        sp.wait_ge(sort_d.rest_out, 16)
                        for s in range(SLOTS):
                            fetch(seg5)(0, s, True)
                    with sp.Fori(1, BATCHES // SLOTS) as i:
                        for half in range(2):
                            store(q, i - 1, half)
                            if q.wide:
                                fetch(q)(i, 2 * half, False)
                                fetch(q)(i, 2 * half + 1, False)
                    for half in range(2):
                        store(q, BATCHES // SLOTS - 1, half)
                elif q is not node4:
                    if q is node1:
                        for s in range(2):
                            load(sort_d, s, 0)
                    view = h_dram[q.number].rearrange("(t p) d -> p t d", p=P)

                    def group(i, full):
                        if q is node3:
                            xs = x[0:N_FULL * P].rearrange("(t p) d -> p t d", p=P)
                            if full:
                                if not is_first(i):
                                    sp.wait_ge(node3.done, i)
                                    sp.nop(nofuse=True)
                                sp.dma_start(xres[:, :, :], xs[:, bass.ds(i * NT, NT), :]).then_inc(s_xload, 16)
                            else:
                                sp.wait_ge(s_hpad, 2)
                                sp.dma_start(xres[:, 0:NT - 1, :], xs[:, N_FULL - NT + 1:N_FULL, :]).then_inc(s_xload, 16)
                                sp.dma_start(xres[0:N_LAST, NT - 1, :], x[N_FULL * P:N, :]).then_inc(s_xload, 16)
                        beside(q, i, range(4), load)
                        sp.wait_ge(q.done, i + 1)
                        sp.nop(nofuse=True)
                        sp.dma_start(view[:, bass.ds(i * NT, NT), :], h[:, bass.ds(i * NT, NT), :]).then_inc(q.out, 16)
                    group(0, True)
                    with sp.Fori(1, NGROUPS - 1) as i:
                        group(i, True)
                    group(NGROUPS - 1, False)
                else:
                    full = out[0:N_FULL * P].rearrange("(t p) d -> p t d", p=P)
                    with sp.Fori(0, NGROUPS - 1) as i:
                        sp.wait_ge(q.done, i + 1)
                        sp.dma_start(full[:, bass.ds(i * NT, NT), :], h[:, bass.ds(i * NT, NT), :]).then_inc(q.out, 16)
                    sp.wait_ge(q.done, NGROUPS)
                    t0 = (NGROUPS - 1) * NT
                    sp.dma_start(full[:, t0:N_FULL, :], h[:, t0:N_FULL, :]).then_inc(q.out, 16)
                    sp.dma_start(out[N_FULL * P:N, :], h[0:N_LAST, N_FULL, :]).then_inc(q.out, 16)
                    sp.wait_ge(q.out, (NGROUPS + 1) * 16)

        @block.gpsimd
        def _(pool):
            pool.iota(iota_tmp[:, 0:P], [[1, P]], base=0, channel_multiplier=0).then_inc(s_iota, 1)
            pool.iota(iota_part_i[:, :], [[0, 1]], base=0, channel_multiplier=1).then_inc(s_iota, 1)
            pool.iota(iota_mark[:, :], [[1, MARKS]], base=0, channel_multiplier=0).then_inc(s_iota, 1)

            def scatter(q, s, use):
                pool.wait_ge(q.load[s], use * 48 + 48)
                pool.wait_ge(q.meta[s], use * 3 + 3)
                pool.nop(nofuse=True)
                for j in range(PB):
                    pool.indirect_dma_start(
                        out=q.table, out_offset=bass.IndirectOffsetOnAxis(ap=ppos[:, s, j:j + 1], axis=0),
                        in_=prow[:, s, j, :], in_offset=None).then_inc(q.out[s], 16)

            def scatter_rest(q):
                pool.wait_ge(q.rest_load, 48)
                pool.wait_ge(q.rest_meta, 3)
                pool.nop(nofuse=True)
                pool.indirect_dma_start(
                    out=q.table, out_offset=bass.IndirectOffsetOnAxis(ap=ppos[0:REST, 0, 0:1], axis=0),
                    in_=prow[0:REST, 0, 0, :], in_offset=None).then_inc(q.rest_out, 16)

            pool.wait_ge(s_zrow["s"], (ROWS // (ZR * P) + 5) * 16)
            sort_batches(pool, sort_s, scatter)
            scatter_rest(sort_s)

            def gather(q):
                def body(i, s, first):
                    n = SLOTS * i + s
                    if q.wide:
                        pool.wait_ge(q.row[s], (i + 1) * 16)
                    else:
                        pool.wait_ge(q.idx, n + 1)
                    if not first:
                        pool.wait_ge(q.mm, (n - SLOTS + 1) * B)
                    elif q is seg5:
                        pool.wait_ge(seg4.mm, CHUNKS - (SLOTS - 1 - s) * B)
                    pool.nop(nofuse=True)
                    for b in range(B):
                        ap = rows[:, s, b, OTHER:OTHER + 1].bitcast(I32) if q.wide else gidx[:, s, b:b + 1]
                        pool.indirect_dma_start(
                            out=got[:, s, b, :], out_offset=None, in_=q.table,
                            in_offset=bass.IndirectOffsetOnAxis(ap=ap, axis=0)).then_inc(q.got[s], 16)
                return body

            def fetch_sums(q, i, u):
                pool.wait_ge(q.idx, i + 1)
                pool.nop(nofuse=True)
                for a, (running, k, bufs) in enumerate(q.sums):
                    for t in range(NT):
                        pool.indirect_dma_start(
                            out=bufs[u][:, t, :], out_offset=None, in_=running,
                            in_offset=bass.IndirectOffsetOnAxis(ap=nidx[:, u, a, t:t + 1], axis=0),
                        ).then_inc(q.sum[u], 16)

            prev = None
            for q in plan:
                if isinstance(q, Pass):
                    if q is seg4:
                        scatter_rest(sort_d)
                    if isinstance(prev, Nodes):
                        pool.wait_ge(prev.out, NGROUPS * 16)
                    batches(pool, gather(q))
                else:
                    if q is node1:
                        pool.wait_ge(s_zrow["d"], (ROWS // (ZR * P)) * 16)
                        for s in range(2):
                            scatter(sort_d, s, 0)
                    segs = {1: [seg1], 2: [seg2], 3: [seg3], 4: [seg1, seg4, seg5]}[q.number]
                    for g in segs:
                        for s in range(2):
                            pool.wait_ge(g.out[s], HALVES * 16)
                    if q is node4:
                        with pool.Fori(0, NGROUPS // 2) as i:
                            for u in range(2):
                                fetch_sums(q, 2 * i + u, u)
                    else:
                        with pool.Fori(0, NGROUPS) as i:
                            fetch_sums(q, i, 0)
                            beside(q, i, range(4), scatter)
                prev = q

        @block.tensor
        def _(pe):
            pe.wait_ge(s_const, 2)
            for n in range(2):
                base = 2 * STEPS * n

                def histogram(j, p, start):
                    pe.wait_ge(s_oh, j + (base + 1))
                    pe.matmul(ps_seg[:, 0, 0:LANES * BINS], ones_bf[:, :], onehot[:, p], start=start,
                              stop=False, skip_group_check=True).then_inc(s_mul, 1)
                histogram(0, 0, True)
                with pe.Fori(0, (STEPS - 1) // 2) as j:
                    histogram(2 * j + 1, 1, False)
                    histogram(2 * j + 2, 0, False)
                pe.wait_ge(s_lane0, n + 1)
                pe.matmul(ps_seg[:, 1, 0:LANES * BINS], ones[0:1, :], lane0[0:1, :, :], start=True,
                          stop=False, skip_group_check=True)

                def rank(j, p):
                    pe.wait_ge(s_oh, j + (base + STEPS + 1))
                    pe.matmul(ps_seg[:, 1, 0:LANES * BINS], upper[:, :], onehot[:, p], start=False,
                              stop=False, skip_group_check=True).then_inc(s_rank, 1)
                    pe.wait_ge(s_read, j + (STEPS * n + 1))
                    pe.matmul(ps_seg[:, 1, 0:LANES * BINS], lower[:, :], onehot[:, p], start=False,
                              stop=False, skip_group_check=True).then_inc(s_mul, 1)
                rank(0, 0)
                with pe.Fori(0, (STEPS - 1) // 2) as j:
                    rank(2 * j + 1, 1)
                    rank(2 * j + 2, 0)
                pe.wait_ge(s_starts, n + 1)
                for a in range(4):
                    mm = pe.matmul(ps_seg[:, a, 0:MARKS], ones[0:T, :], starts[0:T, a, :], start=True, stop=True)
                mm.then_inc(s_bc, 1)
                pe.wait_ge(s_keep, n + 1)

            def seg(q):
                def body(i, s, first):
                    n = SLOTS * i + s
                    pe.wait_ge(q.oh, n + 1)
                    pe.wait_ge(q.got[s], (i + 1) * (16 * B))
                    for b in range(B):
                        if not (first and s == 0):
                            pe.wait_ge(q.run, n * B + (b - B + 1))
                        lhs = seg_oh[:, s, b, :]
                        if q.wide:
                            pe.matmul(ps_seg[:, b, 0:FEAT], lhs, rows[:, s, b, 0:FEAT], start=True, stop=True)
                            mm = pe.matmul(ps_seg[:, b, FEAT:WIDE], lhs, got[:, s, b, :], start=True, stop=True)
                        else:
                            mm = pe.matmul(ps_seg[:, b, 0:D], lhs, got[:, s, b, :], start=True, stop=True)
                        mm.then_inc(q.mm, 1)
                return body

            def layer(q):
                w = wts[q.number - 1]
                with pe.Fori(0, NGROUPS) as i:
                    pe.wait_ge(q.cat, i + 1)
                    for t in range(NT):
                        mm = pe.transpose(ps_t[:, t, :], cat[:, t, :], ident[:, :])
                    mm.then_inc(q.tr, 1)
                    pe.wait_ge(q.ct, i + 1)
                    for t in range(NT):
                        mm = pe.matmul(ps_o[:, t, :], catT[:, t, :], w[:, :], start=True, stop=True)
                    mm.then_inc(q.mm, 1)

            def last(q):
                with pe.Fori(0, NGROUPS) as i:
                    pe.wait_ge(q.cat, i * 2 + 1)
                    for t in range(NT):
                        mm = pe.transpose(ps_t[:, t, :], cat[:, t, :], ident[:, :])
                    mm.then_inc(q.tr, 1)
                    pe.wait_ge(q.ct, i * 3 + 1)
                    pe.wait_ge(q.cat2, i + 1)
                    for t in range(NT):
                        mm = pe.transpose(ps_t[:, t, :], cat2[:, t, :], ident[:, :])
                    mm.then_inc(q.tr, 1)
                    pe.wait_ge(q.ct, i * 3 + 2)
                    for t in range(NT):
                        pe.matmul(ps_o[:, t, :], cat2T[:, t, :], w_n2[:, :], start=True, stop=False,
                                  skip_group_check=True)
                        mm = pe.matmul(ps_o[:, t, 0:D], catT[:, t, :], w_n1[:, :], start=False, stop=True,
                                       skip_group_check=True)
                    mm.then_inc(q.mm, 1)
                    pe.wait_ge(q.cat, i * 2 + 2)
                    for t in range(NT):
                        mm = pe.transpose(ps_t[:, t, :], cat[:, t, :], ident[:, :])
                    mm.then_inc(q.tr, 1)
                    pe.wait_ge(q.ct, i * 3 + 3)
                    for t in range(NT):
                        mm = pe.matmul(ps_o[:, t, 0:D], catT[:, t, :], w_n3[:, :], start=True, stop=True)
                    mm.then_inc(q.mm, 1)

            for q in plan:
                if isinstance(q, Pass):
                    if q is seg5:
                        pe.wait_ge(seg4.run, CHUNKS)
                    batches(pe, seg(q))
                elif q is node4:
                    last(q)
                else:
                    if q is node1:
                        pe.wait_ge(s_wload, 16 * 19)
                    layer(q)

        @block.scalar
        def _(act):
            act.wait_ge(s_const, 2)
            for n, (wg, wl, ws, bb) in enumerate(((Wg1, Wl1, Ws1, b1), (Wg2, Wl2, Ws2, b2), (Wgo, Wlo, Wso, bo))):
                act.dma_start(wts[n][0:D, 0:D], wg).then_inc(s_wload, 16)
                act.dma_start(wts[n][0:D, D:P], ws).then_inc(s_wload, 16)
                act.dma_start(wts[n][D:P, D:P], wl).then_inc(s_wload, 16)
                act.dma_start(bias[n][:, :], bb.unsqueeze(0).to_broadcast([P, D])).then_inc(s_wload, 16)
            act.dma_start(w_n1[:, :], W1t[0:2 * D, :]).then_inc(s_wload, 16)
            act.dma_start(w_n2[0:D, 0:D], W1t[2 * D:3 * D, :]).then_inc(s_wload, 16)
            act.dma_start(w_n2[D:P, D:P], W2t[2 * D:3 * D, :]).then_inc(s_wload, 16)
            act.dma_start(w_n3[:, :], W2t[0:2 * D, :]).then_inc(s_wload, 16)
            act.dma_start(bias_n1[:, :], c1.unsqueeze(0).to_broadcast([P, D])).then_inc(s_wload, 16)
            act.dma_start(bias_n2[:, :], c2.unsqueeze(0).to_broadcast([P, D])).then_inc(s_wload, 16)
            act.dma_start(unit[:, :], stf[0:1, :].to_broadcast([P, D])).then_inc(s_wload, 16)

            def meta(q, s, use):
                if not is_first(use):
                    act.wait_ge(q.out[s], use * (PB * 16))
                elif q is sort_d:
                    act.wait_ge(sort_s.out[s], SORTED)
                    if s == 0:
                        act.wait_ge(sort_s.rest_out, 16)
                cols = bass.ds((2 * use + s) * PB, PB)
                act.copy(prow[:, s, :, LOC], place[q.key][:, cols]).then_inc(q.meta[s], 1)
                act.copy(prow[:, s, :, OTHER].bitcast(I32), keys[q.other][:, cols]).then_inc(q.meta[s], 1)
                act.copy(ppos[:, s, :], pos[q.key][:, cols]).then_inc(q.meta[s], 1)

            def meta_rest(q):
                act.wait_ge(q.out[0], SORTED)
                act.copy(prow[0:REST, 0, 0, LOC:LOC + 1], place[q.key][0:REST, COLS:COLS + 1]).then_inc(q.rest_meta, 1)
                act.copy(prow[0:REST, 0, 0, OTHER:OTHER + 1].bitcast(I32),
                         keys[q.other][0:REST, COLS:COLS + 1]).then_inc(q.rest_meta, 1)
                act.copy(ppos[0:REST, 0, 0:1], pos[q.key][0:REST, COLS:COLS + 1]).then_inc(q.rest_meta, 1)

            act.wait_ge(s_load["d"], 32)
            act.wait_ge(s_ranked, 1)
            sort_batches(act, sort_s, meta)
            meta_rest(sort_s)
            act.wait_ge(s_hpad, 1)
            act.dma_start(h[:, 0:N_FULL, :], x[0:N_FULL * P].rearrange("(t p) d -> p t d", p=P)).then_inc(s_xload, 16)
            act.dma_start(h[0:N_LAST, N_FULL, :], x[N_FULL * P:N, :]).then_inc(s_xload, 16)
            def keep_idx(q):
                def body(i, s, first):
                    n = SLOTS * i + s
                    act.wait_ge(q.row[s], (i + 1) * 16)
                    act.copy(loc_s[:, bass.ds(n * B, B)], rows[:, s, :, LOC]).then_inc(q.tab, 1)
                    act.copy(id_d[:, bass.ds(n * B, B)], rows[:, s, :, OTHER].bitcast(I32)).then_inc(q.tab, 1)
                return body

            def place_idx(q):
                def body(i, s, first):
                    n = SLOTS * i + s
                    if not first:
                        act.wait_ge(q.got[s], i * (16 * B))
                    act.copy(gidx[:, s, :], id_d[:, bass.ds(n * B, B)]).then_inc(q.idx, 1)
                return body

            def sum_idx(q, i, u):
                for a, (running, k, bufs) in enumerate(q.sums):
                    ins = act.copy(nidx[:, u, a, :], lastrow[k][:, bass.ds(i * NT, NT)])
                ins.then_inc(q.idx, 1)

            def transposed(q, i, c, copies):
                act.wait_ge(q.tr, i * copies + (c + 1))
                to = cat2T if c == 1 else catT
                act.copy(to[:, 0:4, :], ps_t[:, 0:4, :])
                act.copy(to[:, 4:NT, :], ps_t[:, 4:NT, :]).then_inc(q.ct, 1)

            def root(q, i):
                act.wait_ge(q.var, i + 1)
                act.activation(nm[:, :, 2], nm[:, :, 1], ACT.Sqrt).then_inc(q.std, 1)

            for q in plan:
                if isinstance(q, Pass):
                    if q is seg1:
                        batches(act, keep_idx(q))
                        act.wait_ge(q.tab, 2 * BATCHES)
                    elif not q.wide:
                        if q is seg4:
                            meta_rest(sort_d)
                        batches(act, place_idx(q))
                elif q is not node4:
                    if q is node1:
                        act.wait_ge(s_ranked, 2)
                        for s in range(2):
                            meta(sort_d, s, 0)

                    def group(i):
                        if not is_first(i):
                            act.wait_ge(q.sum[0], i * (16 * NT))
                        sum_idx(q, i, 0)
                        beside(q, i, range(2), meta)
                        transposed(q, i, 0, 1)
                        act.wait_ge(q.neg, i + 1)
                        act.activation(nb[:, :, :], nb[:, :, :], ACT.Exp).then_inc(q.exp, 1)
                        if q is node3:
                            root(q, i)
                        beside(q, i, range(2, 4), meta)
                    group(0)
                    with act.Fori(1, NGROUPS) as i:
                        group(i)
                else:
                    def work(i):
                        for c in range(3):
                            transposed(q, i, c, 3)
                        root(q, i)
                    for u in range(2):
                        sum_idx(q, u, u)
                    with act.Fori(0, NGROUPS // 2 - 1) as i:
                        for u in range(2):
                            work(2 * i + u)
                            act.wait_ge(q.sum[u], i * (16 * NT * 3) + 16 * NT * 3)
                            sum_idx(q, 2 * i + (2 + u), u)
                    for u in range(2):
                        work(NGROUPS - 2 + u)

        @block.vector
        def _(dve):
            dve.memset(zeros[:, :], 0.0).then_inc(s_zero, 1)
            for k in "sd":
                dve.memset(keys[k][:, COLS:KEYC], T * P).then_inc(s_pad, 1)
            dve.wait_ge(s_pad, 2)
            dve.memset(prow[:, :, :, ONE:ONE + 1], 1.0)
            dve.memset(prow[:, :, :, OTHER + 1:ROW], 0.0).then_inc(s_const, 1)
            dve.memset(ones_bf[:, :], 1.0)
            dve.memset(ones[:, :], 1.0)
            for wmat in (*wts, w_n2):
                dve.memset(wmat[:, :], 0.0)
            dve.memset(loc_s[:, CHUNKS:CHUNKS + B], 0.0)
            dve.memset(run[:, :, :, :], 0.0)
            dve.wait_ge(s_iota, 3)
            dve.tensor_copy(iota_part[:, :], iota_part_i[:, :])
            chain(dve, dve.tensor_copy(iota_row[:, :], iota_tmp[:, :]))
            dve.tensor_copy(iota_bin[:, :], iota_tmp[:, 0:BINS])
            dve.tensor_scalar(iota_loc[:, :], iota_row[:, :], 1.0, None, ALU.add)
            dve.tensor_scalar(ident[:, :], iota_row[:, :], iota_part[:, 0:1], None, ALU.is_equal)
            dve.tensor_scalar(upper[:, :], iota_row[:, :], iota_part[:, 0:1], None, ALU.is_gt)
            dve.tensor_scalar(lower[:, :], iota_row[:, :], iota_part[:, 0:1], None, ALU.is_le).then_inc(s_const, 1)
            dve.wait_ge(s_const, 2)

            def bins_of(j, p):
                dve.tensor_tensor(
                    onehot[:, p], tid[:, bass.ds(j * LANES, LANES)].unsqueeze(2).to_broadcast([P, LANES, BINS]),
                    iota_bin[:, :].unsqueeze(1).to_broadcast([P, LANES, BINS]), ALU.is_equal).then_inc(s_oh, 1)

            def ranking(n, k):
                base = 2 * STEPS * n
                dve.wait_ge(s_load[k], 32)
                chain(dve, dve.tensor_scalar(bits[:, :], keys[k][:, :], P - 1, None, ALU.bitwise_and))
                chain(dve, dve.tensor_scalar(place[k][:, :], bits[:, :], 1.0, None, ALU.add))
                chain(dve, dve.tensor_scalar(bits[:, :], keys[k][:, :], 7, None, ALU.logical_shift_right))
                chain(dve, dve.tensor_copy(tid[:, :], bits[:, :]))

                for j in range(2):
                    bins_of(j, j)

                def more(j, p):
                    dve.wait_ge(s_mul, j + (base - 1))
                    bins_of(j, p)
                with dve.Fori(1, (STEPS - 1) // 2) as j:
                    more(2 * j, 0)
                    more(2 * j + 1, 1)
                more(STEPS - 1, 0)
                dve.wait_ge(s_mul, base + STEPS)
                chain(dve, dve.tensor_copy(prod[:, :, :], ps_seg[:, 0, 0:LANES * BINS].rearrange(
                    "p (l b) -> p l b", l=LANES)))
                chain(dve, dve.tensor_reduce(count[:, :], prod[:, :, :].rearrange("p l b -> p b l"), AX.X, ALU.add))
                chain(dve, dve.tensor_scalar(nchunk_i[:, :], count[:, :], float(P - 1), None, ALU.add))
                chain(dve, dve.tensor_scalar(nchunk_i[:, :], nchunk_i[:, :], 7, None, ALU.logical_shift_right))
                chain(dve, dve.tensor_copy(nchunk[:, :], nchunk_i[:, :]))
                chain(dve, dve.tensor_tensor_scan(cend[:, :], nchunk[:, :], nchunk[:, :], 0.0, ALU.add, ALU.bypass))
                chain(dve, dve.tensor_tensor(cstart[:, :], cend[:, :], nchunk[:, :], ALU.subtract))
                chain(dve, dve.tensor_scalar(filled[:, :], nchunk[:, :], 1.0, None, ALU.min))
                chain(dve, dve.tensor_scalar(lane0[:, 0, :], cstart[:, :], float(P), None, ALU.mult))
                for l in range(1, LANES):
                    ins = dve.tensor_tensor(lane0[:, l, :], lane0[:, l - 1, :], prod[:, l - 1, :], ALU.add)
                    if l < LANES - 1:
                        chain(dve, ins)
                ins.then_inc(s_lane0, 1)
                dve.wait_ge(s_lane0, n + 1)

                def position(j, p, last):
                    if not last:
                        dve.wait_ge(s_mul, j + (base + STEPS))
                        bins_of(j + 1, 1 - p)
                    dve.wait_ge(s_rank, j + (STEPS * n + 1))
                    dve.tensor_tensor(prod[:, :, :], onehot[:, p],
                                      ps_seg[:, 1, 0:LANES * BINS].rearrange("p (l b) -> p l b", l=LANES),
                                      ALU.mult).then_inc(s_read, 1)
                    dve.wait_ge(s_read, j + (STEPS * n + 1))
                    dve.tensor_reduce(pos[k][:, bass.ds(j * LANES, LANES)], prod[:, :, :], AX.X,
                                      ALU.add).then_inc(s_prod, 1)
                    dve.wait_ge(s_prod, j + (STEPS * n + 1))
                bins_of(0, 0)
                with dve.Fori(0, (STEPS - 1) // 2) as j:
                    position(2 * j, 0, False)
                    position(2 * j + 1, 1, False)
                position(STEPS - 1, 0, True)
                dve.wait_ge(s_mul, base + 2 * STEPS)
                dve.memset(binsq[:, :], 0.0).then_inc(s_ranked, 1)
                dve.wait_ge(s_ranked, n + 1)

                for row, col in ((cstart, startcol), (filled, fillcol)):
                    chain(dve, dve.tensor_tensor(binsq[:, :], row[:, :], ident[:, 0:BINS], ALU.mult))
                    chain(dve, dve.tensor_reduce(col[:, :], binsq[:, :], AX.X, ALU.add))
                for a in range(4):
                    dve.tensor_scalar(starts[:, a, :], iota_mark[:, :], float(MARKS * a), startcol[:, 0:1],
                                      ALU.add, ALU.is_equal).then_inc(s_v, 1)
                vcount[0] += 4
                dve.wait_ge(s_v, vcount[0])
                dve.tensor_scalar(starts[:, :, :], starts[:, :, :], fillcol[:, 0:1], None, ALU.mult).then_inc(s_starts, 1)
                dve.wait_ge(s_bc, n + 1)
                dve.tensor_scalar(keep[k][:, :].rearrange("p (a c) -> p a c", a=4), ps_seg[:, :, 0:MARKS],
                                  -1.0, 1.0, ALU.mult, ALU.add).then_inc(s_keep, 1)
                chain(dve, dve.tensor_tensor(binsq[:, :], cend[:, :], filled[:, :], ALU.mult))
                chain(dve, dve.tensor_scalar(lastrow[k][:, :], binsq[:, 0:T], float(P), iota_part[:, 0:1],
                                             ALU.mult, ALU.add))

            ranking(0, "s")
            ranking(1, "d")
            dve.wait_ge(s_zrow["d"], (ROWS // (ZR * P)) * 16)
            dve.memset(h[:, N_FULL, :], 0.0).then_inc(s_hpad, 1)
            dve.wait_ge(s_hpad, 1)

            def onehots(q, i, s, first):
                n = SLOTS * i + s
                if not first:
                    dve.wait_ge(q.mm, (n - SLOTS + 1) * B)
                if q.wide:
                    dve.wait_ge(q.row[s], (i + 1) * 16)
                    loc = rows[:, s, :, LOC:LOC + 1]
                else:
                    loc = loc_s[:, bass.ds(n * B, B)].unsqueeze(2)
                dve.tensor_tensor(seg_oh[:, s], loc.to_broadcast([P, B, P]),
                                  iota_loc[:, :].unsqueeze(1).to_broadcast([P, B, P]),
                                  ALU.is_equal).then_inc(q.oh, 1)

            def running(q, i, s, first):
                n = SLOTS * i + s
                w = q.width
                half, at = s // 2, (s % 2) * B
                if s % 2 == 0 and not first:
                    dve.wait_ge(q.out[half], i * 16)
                for b in range(B):
                    dve.wait_ge(q.mm, n * B + (b + 1))
                    if not (first and s == 0 and b == 0):
                        dve.wait_ge(q.run, n * B + b)
                    before = run[:, half, at + b - 1, 0:w] if at + b else run[:, 1 - half, 2 * B - 1, 0:w]
                    dve.scalar_tensor_tensor(
                        run[:, half, at + b, 0:w], before, keep[q.key][:, bass.ds(n * B + b, 1)],
                        ps_seg[:, b, 0:w], ALU.mult, ALU.add).then_inc(q.run, 1)

            def seg(q):
                def body(i, first, last):
                    for s in range(SLOTS):
                        if s < SLOTS - 1:
                            onehots(q, i, s + 1, first)
                        elif not last:
                            onehots(q, i + 1, 0, False)
                        running(q, i, s, first)
                onehots(q, 0, 0, True)
                body(0, True, False)
                with dve.Fori(1, BATCHES // SLOTS - 1) as i:
                    body(i, False, False)
                body(BATCHES // SLOTS - 1, False, True)

            def bc(ap):
                return ap.unsqueeze(2).to_broadcast([P, NT, D])

            class Steps:

                def __init__(self, q, i, per):
                    self.q, self.i, self.per, self.n = q, i, per, 0

                def __call__(self, ins):
                    self.n += 1
                    ins.then_inc(self.q.v, 1)
                    dve.wait_ge(self.q.v, self.i * self.per + self.n)

            def layernorm(q, step, i):
                hs = h[:, bass.ds(i * NT, NT), :]
                step(dve.tensor_reduce(nm[:, :, 0], na[:, :, :], AX.X, ALU.add))
                step(dve.tensor_scalar(nm[:, :, 0], nm[:, :, 0], 1.0 / D, None, ALU.mult))
                step(dve.tensor_tensor(na[:, :, :], na[:, :, :], bc(nm[:, :, 0]), ALU.subtract))
                step(dve.tensor_tensor(nb[:, :, :], na[:, :, :], na[:, :, :], ALU.mult))
                step(dve.tensor_reduce(nm[:, :, 1], nb[:, :, :], AX.X, ALU.add))
                dve.tensor_scalar(nm[:, :, 1], nm[:, :, 1], 1.0 / D, EPS, ALU.mult, ALU.add).then_inc(q.var, 1)
                dve.wait_ge(q.std, i + 1)
                step(dve.reciprocal(nm[:, :, 3], nm[:, :, 2]))
                dve.tensor_tensor(hs, na[:, :, :], bc(nm[:, :, 3]), ALU.mult).then_inc(q.done, 1)
                dve.wait_ge(q.done, i + 1)

            def layer(q):
                wide = q is node1
                normed = q is node3
                per = (4 if wide else 0) + 5 + (8 if normed else 0)
                def group(i):
                    step = Steps(q, i, per)
                    ts = bass.ds(i * NT, NT)
                    hs = h[:, ts, :]
                    dve.wait_ge(q.sum[0], (i + 1) * (16 * NT))
                    if wide:
                        step(dve.tensor_scalar(linked[:, ts], sum_a[:, :, ONE], 1.0, None, ALU.min))
                        step(dve.tensor_scalar(nm[:, :, 4], sum_a[:, :, ONE], 1.0, None, ALU.max))
                        step(dve.reciprocal(nm[:, :, 5], nm[:, :, 4]))
                        step(dve.tensor_scalar(inv[:, ts], nm[:, :, 5], 1.0, None, ALU.mult))
                        agg = sum_a[:, :, FEAT:WIDE]
                    else:
                        agg = sum_c[:, :, :]
                    step(dve.tensor_scalar(cat[:, :, 0:D], hs, 1.0, None, ALU.mult))
                    dve.tensor_tensor(cat[:, :, D:P], agg, bc(inv[:, ts]), ALU.mult).then_inc(q.cat, 1)
                    dve.wait_ge(q.mm, i + 1)
                    step(dve.tensor_tensor(na[:, :, :], ps_o[:, 0:NT, 0:D],
                                           bias[q.number - 1][:, :].unsqueeze(1).to_broadcast([P, NT, D]), ALU.add))
                    step(dve.tensor_tensor(nb[:, :, :], ps_o[:, 0:NT, D:P], bc(linked[:, ts]), ALU.mult))
                    step(dve.tensor_tensor(na[:, :, :], na[:, :, :], nb[:, :, :], ALU.add))
                    dve.tensor_scalar(nb[:, :, :], na[:, :, :], 0.0, None, ALU.min).then_inc(q.neg, 1)
                    step(dve.tensor_scalar(cat[:, :, 0:D], na[:, :, :], 0.0, -1.0, ALU.max, ALU.add))
                    dve.wait_ge(q.exp, i + 1)
                    if not normed:
                        dve.tensor_tensor(hs, cat[:, :, 0:D], nb[:, :, :], ALU.add).then_inc(q.done, 1)
                        dve.wait_ge(q.done, i + 1)
                    else:
                        step(dve.tensor_tensor(na[:, :, :], cat[:, :, 0:D], nb[:, :, :], ALU.add))
                        final = isinstance(i, int) and i == NGROUPS - 1
                        dve.wait_ge(s_xload, i * 16 + (64 if final else 48))
                        step(dve.tensor_tensor(na[:, :, :], na[:, :, :], xres[:, :, :], ALU.add))
                        layernorm(q, step, i)
                    assert step.n == per, step.n

                group(0)
                with dve.Fori(1, NGROUPS - 1) as i:
                    group(i)
                if normed:
                    dve.memset(xres[:, NT - 1, :], 0.0).then_inc(s_hpad, 1)
                group(NGROUPS - 1)

            def last(q):
                with dve.Fori(0, NGROUPS // 2) as half:
                    for u, (sum_a, sum_b, sum_c) in enumerate(zip(*(bufs for _, _, bufs in q.sums))):
                        last_group(q, half, u, sum_a, sum_b, sum_c)

            def last_group(q, half, u, sum_a, sum_b, sum_c):
                    i = 2 * half + u
                    step = Steps(q, i, 19)
                    ts = bass.ds(i * NT, NT)
                    hs = h[:, ts, :]
                    dve.wait_ge(q.sum[u], half * (16 * NT * 3) + 16 * NT * 3)
                    u = unit[:, :].unsqueeze(1).to_broadcast([P, NT, D])
                    step(dve.tensor_tensor(na[:, :, :], sum_c[:, :, :], sum_b[:, :, FEAT:WIDE], ALU.add))
                    step(dve.tensor_tensor(cat[:, :, 0:D], na[:, :, :], hs, ALU.add))
                    step(dve.tensor_tensor(sum_a[:, :, 0:FEAT], sum_a[:, :, 0:FEAT], sum_b[:, :, 0:FEAT], ALU.add))
                    dve.tensor_copy(cat[:, :, D:P], sum_a[:, :, EF:EF + D]).then_inc(q.cat, 1)
                    step(dve.tensor_scalar(nm[:, :, 4], sum_a[:, :, ONE], 1.0, None, ALU.add))
                    step(dve.reciprocal(nm[:, :, 5], nm[:, :, 4]))
                    step(dve.tensor_tensor(cat2[:, :, 0:D], sum_a[:, :, ET:ET + D], u, ALU.add))
                    step(dve.tensor_tensor(nb[:, :, :], sum_a[:, :, STF:STF + D], u, ALU.add))
                    dve.tensor_tensor(cat2[:, :, D:P], nb[:, :, :], bc(nm[:, :, 5]), ALU.mult).then_inc(q.cat2, 1)
                    dve.wait_ge(q.cat2, i + 1)
                    step(dve.tensor_tensor(nb[:, :, :], bias_n1[:, :].unsqueeze(1).to_broadcast([P, NT, D]),
                                           bc(nm[:, :, 4]), ALU.mult))
                    dve.wait_ge(q.mm, i * 2 + 1)
                    step(dve.tensor_tensor(na[:, :, :], ps_o[:, 0:NT, 0:D], nb[:, :, :], ALU.add))
                    step(dve.tensor_scalar(cat[:, :, D:P], hs, 1.0, None, ALU.mult))
                    dve.tensor_scalar(cat[:, :, 0:D], na[:, :, :], 0.0, None, ALU.max).then_inc(q.cat, 1)
                    dve.wait_ge(q.mm, i * 2 + 2)
                    step(dve.tensor_tensor(na[:, :, :], ps_o[:, 0:NT, 0:D],
                                           bias_n2[:, :].unsqueeze(1).to_broadcast([P, NT, D]), ALU.add))
                    step(dve.tensor_tensor(na[:, :, :], na[:, :, :], ps_o[:, 0:NT, D:P], ALU.add))
                    step(dve.tensor_tensor(na[:, :, :], na[:, :, :], hs, ALU.add))
                    layernorm(q, step, i)
                    assert step.n == 19, step.n

            for q in plan:
                if isinstance(q, Pass):
                    if q is seg2:
                        dve.wait_ge(seg1.tab, 2 * BATCHES)
                    if q is seg5:
                        for s in range(2):
                            dve.wait_ge(seg4.out[s], HALVES * 16)
                    seg(q)
                elif q is node4:
                    last(q)
                else:
                    if q is node1:
                        dve.wait_ge(s_wload, 16 * 19)
                        dve.wait_ge(s_xload, 32)
                    layer(q)


_INS = ["x", "src", "dst", "edge_attr_64", "edge_attr_64_n2", "edge_attr_64_n3",
        "L0_gnn_Wg1", "L0_gnn_Wl1", "L0_gnn_Ws1", "L0_gnn_b1", "L0_gnn_Wg2", "L0_gnn_Wl2", "L0_gnn_Ws2", "L0_gnn_b2",
        "L0_gnn_Wgo", "L0_gnn_Wlo", "L0_gnn_Wso", "L0_gnn_bo", "L1_gnn_W1", "L1_gnn_b1", "L1_gnn_W2", "L1_gnn_b2"]


def kernel(**inputs):
    import concourse.bacc as bacc
    from concourse.bass_utils import run_bass_kernel_spmd

    nc = bacc.Bacc("TRN2", target_bir_lowering=False, num_devices=1)
    arrays, args = {}, []
    for name in _INS:
        a = np.asarray(inputs[name])
        if name in ("L1_gnn_W1", "L1_gnn_W2"):
            a = a.T
        a = np.ascontiguousarray(a)
        arrays[f"in_{name}"] = a
        args.append(nc.dram_tensor(f"in_{name}", a.shape, mybir.dt.from_np(a.dtype), kind="ExternalInput").ap())
    args.append(nc.dram_tensor("out_x", (N, D), F32, kind="ExternalOutput").ap())
    build(nc, *args)
    r = run_bass_kernel_spmd(nc, [arrays], core_ids=[0])
    return r.results[0]["out_x"]
```

```python
from contextlib import ExitStack

import numpy as np

import concourse.bass as bass
from concourse import mybir

ALU = mybir.AluOpType
ACT = mybir.ActivationFunctionType
AX = mybir.AxisListType
F32 = mybir.dt.float32
BF16 = mybir.dt.bfloat16
I32 = mybir.dt.int32

P = 128
D = 64
N = 12500
E = 200000
T = -(-N // P)
N_FULL = N // P
N_LAST = N - N_FULL * P
EPS = 1e-5

COLS = E // P
REST = E - COLS * P
LANES = 5
STEPS = -(-(COLS + 1) // LANES)
KEYC = STEPS * LANES
BINS = T + 1

B = 4
SLOTS = 4
CHUNKS = -(-(E // P + T + 1) // (SLOTS * B)) * (SLOTS * B)
BATCHES = CHUNKS // B
ROWS = CHUNKS * P

EF, ET, STF, ONE, LOC, OTHER, ROW = 0, D, 2 * D, 3 * D, 3 * D + 1, 3 * D + 2, 3 * D + 4
FEAT = ONE + 1
WIDE = FEAT + D

PB = 11
PBATCHES = COLS // PB
NT = 7
NGROUPS = T // NT
MARKS = CHUNKS // 4

BESIDE = {1: (0, 4), 2: (4 * NGROUPS, 2), 3: (6 * NGROUPS, 4)}
TAIL = 10 * NGROUPS

BULK = 8
UNUSED = CHUNKS - -(-E // P)
BULKS = -(-UNUSED // BULK)
CLEARS = 3 * (PBATCHES // 4)
BEHIND = BULKS * BULK + CLEARS
assert CLEARS >= T
assert STEPS % 4 == 1
AHEAD = -(-2 * PB // LANES)

assert COLS % (2 * PB) == 0 and T % NT == 0 and NGROUPS % 2 == 0
assert TAIL + 2 == PBATCHES and PBATCHES // 2 % 2 == 1


def is_first(i):
    return isinstance(i, int) and i == 0


def build(nc, x, src, dst, ef, stf, et, Wg1, Wl1, Ws1, b1, Wg2, Wl2, Ws2, b2, Wgo, Wlo, Wso, bo,
          W1t, c1, W2t, c2, out):
    with ExitStack() as ctx:
        early = ExitStack()

        def sb(name, shape, dt=F32):
            return ctx.enter_context(nc.sbuf_tensor(name, shape, dt))

        def sb_early(name, shape, dt=F32):
            return early.enter_context(nc.sbuf_tensor(name, shape, dt))

        def sem(name):
            return ctx.enter_context(nc.semaphore(name))

        def dram(name, shape):
            return nc.dram_tensor(name, shape, F32).ap()

        sorted_s = dram("sorted_by_src", (ROWS + BEHIND * P, ROW))
        sorted_d = dram("sorted_by_dst", (ROWS + BEHIND * P, ROW))
        h_dram = [None, dram("h1", (T * P, D)), dram("h2", (T * P, D)), dram("x1", (T * P, D))]
        run_wide_s = dram("run_wide_s", ((CHUNKS + 1) * P, WIDE))
        run_wide_d = dram("run_wide_d", ((CHUNKS + 1) * P, WIDE))
        run_thin = [dram(f"run_thin{i}", ((CHUNKS + 1) * P, D)) for i in range(3)]

        ps_seg = ctx.enter_context(nc.psum_tensor("ps_seg", [P, B, 512], F32))
        ps_t = ctx.enter_context(nc.psum_tensor("ps_t", [P, 8, P], F32))
        ps_o = ctx.enter_context(nc.psum_tensor("ps_o", [P, 8, P], F32))

        bin_lane = sb("bin_lane", [P, BINS, LANES], BF16)
        iota_loc = sb("iota_loc", [P, P], BF16)
        iota_row = sb("iota_row", [P, P])
        iota_part = sb("iota_part", [P, 1])
        iota_part_i = sb("iota_part_i", [P, 1], I32)
        upper = sb("upper", [P, P], BF16)
        lower = sb("lower", [P, P], BF16)
        ones_bf = sb("ones_bf", [P, P], BF16)
        ones = sb("ones", [P, P])
        ident = sb("ident", [P, P])
        keep = {k: sb(f"keep_{k}", [P, CHUNKS], BF16) for k in "sd"}
        zeros = sb("zeros", [P, WIDE])
        clear_at = {k: sb(f"clear_at_{k}", [P, CLEARS], I32) for k in "sd"}
        bulk_at = {k: sb(f"bulk_at_{k}", [P, BULKS], I32) for k in "sd"}
        lastrow = {k: sb(f"lastrow_{k}", [P, T], I32) for k in "sd"}

        wts = [sb(f"wts{i}", [P, P]) for i in range(3)]
        bias = [sb(f"bias{i}", [P, D]) for i in range(3)]
        w_n1 = sb("w_n1", [P, D])
        w_n2 = sb("w_n2", [P, P])
        w_n3 = sb("w_n3", [P, D])
        bias_n1 = sb("bias_n1", [P, D])
        bias_n2 = sb("bias_n2", [P, D])
        unit = sb("unit", [P, D])

        keys = {k: sb(f"keys_{k}", [P, KEYC], I32) for k in "sd"}
        place = {k: sb(f"place_{k}", [P, KEYC], BF16) for k in "sd"}
        pos = {k: sb(f"pos_{k}", [P, KEYC]) for k in "sd"}
        prow = sb("prow", [P, 2, PB, ROW])
        ppos = sb("ppos", [P, 2, PB], I32)

        rows = sb("rows", [P, SLOTS, B, ROW])
        seg_oh = sb("seg_oh", [P, SLOTS, B, P])
        got = sb("got", [P, SLOTS, B, D])
        gidx = sb("gidx", [P, SLOTS, B], I32)
        loc_s = sb("loc_s", [P, CHUNKS + B], BF16)
        id_d = sb("id_d", [P, CHUNKS], I32)
        run = sb("run", [P, 2, 2 * B, WIDE])

        inv = sb("inv", [P, T])
        linked = sb("linked", [P, T])
        sum_a = sb("sum_a", [P, NT, WIDE])
        sum_b = sb("sum_b", [P, NT, WIDE])
        sum_c = sb("sum_c", [P, NT, D])
        flat = run[:, :, :, :].rearrange("p a b w -> p (a b w)")
        spare_a = flat[:, 0:NT * WIDE].rearrange("p (t w) -> p t w", w=WIDE)
        spare_b = flat[:, NT * WIDE:2 * NT * WIDE].rearrange("p (t w) -> p t w", w=WIDE)
        spare_c = flat[:, 2 * NT * WIDE:2 * NT * WIDE + NT * D].rearrange("p (t w) -> p t w", w=D)
        cat = sb("cat", [P, NT, P])
        cat2 = sb("cat2", [P, NT, P])
        catT = sb("catT", [P, NT, P])
        cat2T = sb("cat2T", [P, NT, P])
        na = sb("na", [P, NT, D])
        nb = sb("nb", [P, NT, D])
        nm = sb("nm", [P, NT, 8])
        xres = sb("xres", [P, NT, D])
        nm2 = sb("nm2", [P, NT, 8])
        flat_oh = seg_oh[:, :, :, :].rearrange("p s b k -> p (s b k)")
        flat_got = got[:, :, :, :].rearrange("p s b d -> p (s b d)")
        cats = [cat[:, :, :], flat_oh[:, 0:NT * P].rearrange("p (t k) -> p t k", k=P)]
        cats2 = [cat2[:, :, :], flat_oh[:, NT * P:2 * NT * P].rearrange("p (t k) -> p t k", k=P)]
        nas = [na[:, :, :], flat_got[:, 0:NT * D].rearrange("p (t d) -> p t d", d=D)]
        nbs = [nb[:, :, :], flat_got[:, NT * D:2 * NT * D].rearrange("p (t d) -> p t d", d=D)]
        nms = [nm[:, :, :], nm2[:, :, :]]
        products = [ps_o[:, :, :], ps_seg[:, 0:2, :].rearrange("p a (t k) -> p (a t) k", k=P)]

        iota_tmp = sb_early("iota_tmp", [P, P], I32)
        iota_mark = sb_early("iota_mark", [P, MARKS], I32)
        bits = sb_early("bits", [P, KEYC], I32)
        tid = sb_early("tid", [P, KEYC], BF16)
        onehot = sb_early("onehot", [P, 4, BINS, LANES], BF16)
        prod = sb_early("prod", [P, 2, BINS, LANES])
        lane0 = sb_early("lane0", [P, 2, BINS, LANES])
        iota_clear_i = sb_early("iota_clear_i", [P, CLEARS], I32)
        own, block_at, block_in = (sb_early(n, [P, CLEARS]) for n in ("own", "block_at", "block_in"))
        bulk_first = sb_early("bulk_first", [P, BULKS])
        count, nchunk, cend, cstart, filled, binsq = (
            sb_early(n, [P, BINS]) for n in ("count", "nchunk", "cend", "cstart", "filled", "binsq"))
        nchunk_i = sb_early("nchunk_i", [P, BINS], I32)
        startcol = sb_early("startcol", [P, 1])
        fillcol = sb_early("fillcol", [P, 1])
        starts = sb_early("starts", [P, 4, MARKS])
        early.close()
        h = sb("h", [P, T, D])

        s_const = sem("s_const")
        s_iota = sem("s_iota")
        s_load = {k: sem(f"s_load_{k}") for k in "sd"}
        s_wload = sem("s_wload")
        s_xload = sem("s_xload")
        s_hpad = sem("s_hpad")
        s_zero = sem("s_zero")
        s_zrow = {k: sem(f"s_zrow_{k}") for k in "sd"}
        s_clear_at = sem("s_clear_at")
        s_pad = sem("s_pad")
        s_v = sem("s_v")
        s_oh = sem("s_oh")
        s_mul = sem("s_mul")
        s_lane0 = sem("s_lane0")
        s_rank = sem("s_rank")
        s_read = sem("s_read")
        s_prod = sem("s_prod")
        s_ranked = sem("s_ranked")
        s_starts = sem("s_starts")
        s_bc = sem("s_bc")
        s_keep = sem("s_keep")
        s_last = sem("s_last")

        vcount = [0]

        def chain(dve, ins):
            vcount[0] += 1
            ins.then_inc(s_v, 1)
            dve.wait_ge(s_v, vcount[0])

        block = ctx.enter_context(nc.Block())

        class Sort:

            def __init__(self, name, key, other, table):
                self.key, self.other, self.table = key, other, table
                self.load = [sem(f"{name}_load{i}") for i in range(2)]
                self.meta = [sem(f"{name}_meta{i}") for i in range(2)]
                self.out = [sem(f"{name}_out{i}") for i in range(2)]
                self.rest_load, self.rest_meta, self.rest_out = (sem(f"{name}_rest{i}") for i in range(3))

        sort_s = Sort("sort_s", "s", "d", sorted_s)
        sort_d = Sort("sort_d", "d", "s", sorted_d)
        SORTED = (PBATCHES // 2) * (PB * 16)

        class Pass:

            def __init__(self, name, key, table, running, table_rows):
                self.key, self.table, self.running, self.table_rows = key, table, running, table_rows
                self.wide = table_rows is not None
                self.width = WIDE if self.wide else D
                if self.wide:
                    self.row = [sem(f"{name}_row{i}") for i in range(SLOTS)]
                else:
                    self.idx = sem(f"{name}_idx")
                if name == "seg1":
                    self.tab = sem(f"{name}_tab")
                self.got = [sem(f"{name}_got{i}") for i in range(SLOTS)]
                self.oh = sem(f"{name}_oh")
                self.mm = sem(f"{name}_mm")
                self.run = sem(f"{name}_run")
                self.out = [sem(f"{name}_out{i}") for i in range(2)]

        HALVES = BATCHES // 4

        seg1 = Pass("seg1", "s", x, run_wide_s, sorted_s)
        seg2 = Pass("seg2", "s", h_dram[1], run_thin[0], None)
        seg3 = Pass("seg3", "s", h_dram[2], run_thin[1], None)
        seg4 = Pass("seg4", "s", h_dram[3], run_thin[2], None)
        seg5 = Pass("seg5", "d", h_dram[3], run_wide_d, sorted_d)

        class Nodes:

            def __init__(self, name, number, sums):
                self.number, self.sums = number, sums
                self.sum = [sem(f"{name}_sum{i}") for i in range(2 if number == 4 else 1)]
                self.cat = sem(f"{name}_cat")
                self.tr = sem(f"{name}_tr")
                self.ct = sem(f"{name}_ct")
                self.mm = sem(f"{name}_mm")
                if number == 4:
                    self.cat2 = sem(f"{name}_cat2")
                    self.cat3 = sem(f"{name}_cat3")
                    self.front = sem(f"{name}_front")
                else:
                    self.neg = sem(f"{name}_neg")
                    self.exp = sem(f"{name}_exp")
                if number >= 3:
                    self.var = sem(f"{name}_var")
                    self.std = sem(f"{name}_std")
                self.v = sem(f"{name}_v")
                self.done = sem(f"{name}_done")
                self.out = sem(f"{name}_out")

        node1 = Nodes("node1", 1, [(run_wide_s, "s", [sum_a])])
        node2 = Nodes("node2", 2, [(run_thin[0], "s", [sum_c])])
        node3 = Nodes("node3", 3, [(run_thin[1], "s", [sum_c])])
        node4 = Nodes("node4", 4, [(run_wide_s, "s", [sum_a, spare_a]), (run_wide_d, "d", [sum_b, spare_b]),
                                   (run_thin[2], "s", [sum_c, spare_c])])
        plan = [seg1, node1, seg2, node2, seg3, node3, seg4, seg5, node4]

        def batches(eng, body):
            for s in range(SLOTS):
                body(0, s, True)
            with eng.Fori(1, BATCHES // SLOTS) as i:
                for s in range(SLOTS):
                    body(i, s, False)

        def sort_batches(eng, q, body):
            for s in range(2):
                body(q, s, 0)
            with eng.Fori(1, PBATCHES // 2) as i:
                for s in range(2):
                    body(q, s, i)

        def store(eng, q, i, half):
            n = SLOTS * i + 2 * half
            eng.wait_ge(q.run, (n + 2) * B)
            eng.nop(nofuse=True)
            eng.dma_start(q.running.rearrange("(c p) w -> p c w", p=P)[:, bass.ds(n * B + 1, 2 * B), :],
                          run[:, half, :, 0:q.width]).then_inc(q.out[half], 16)

        def ahead(q, body):
            for s in range(2):
                body(sort_d, s, BESIDE[q.number][0] // 2)

        def tail(body):
            for s in range(2):
                body(sort_d, s, TAIL // 2)

        def clear(eng, k, table, i):
            at = eng.value_load(clear_at[k][0:1, bass.ds(i, 1)], min_val=0, max_val=ROWS + (BEHIND - 1) * P)
            eng.dma_start(table[bass.ds(at, P), :], zeros[:, 0:ROW]).then_inc(s_zrow[k], 16)

        def clear_bulk(eng, k, table, i):
            at = eng.value_load(bulk_at[k][0:1, bass.ds(i, 1)], min_val=0, max_val=ROWS + (BULKS - 1) * BULK * P)
            eng.dma_start(table[bass.ds(at, BULK * P), :].rearrange("(b p) w -> p b w", p=P),
                          zeros[:, 0:ROW].unsqueeze(1).to_broadcast([P, BULK, ROW])).then_inc(s_zrow[k], 16)

        def beside(q, i, js, body):
            base, per = BESIDE[q.number]
            last = isinstance(i, int) and i == NGROUPS - 1
            for j in js:
                if j < (per - 2 if last else per):
                    body(sort_d, j % 2, i * (per // 2) + (base // 2 + 1 + j // 2))

        @block.sync
        def _(sp):
            for k, a in (("s", src), ("d", dst)):
                sp.wait_ge(s_pad, 2)
                sp.dma_start(keys[k][:, 0:COLS], a[0:P * COLS].rearrange("(p c) -> p c", p=P)).then_inc(s_load[k], 16)
                sp.dma_start(keys[k][0:REST, COLS:COLS + 1],
                             a[P * COLS:E].rearrange("(p c) -> p c", c=1)).then_inc(s_load[k], 16)
            sp.wait_ge(s_zero, 1)
            for running in (run_wide_s, run_wide_d, *run_thin):
                sp.dma_start(running[0:P, :], zeros[:, 0:running.shape[1]]).then_inc(s_zrow["s"], 16)

            def load(q, s, use):
                if not is_first(use):
                    sp.wait_ge(q.out[s], use * (PB * 16))
                elif q is sort_d:
                    sp.wait_ge(sort_s.out[s], SORTED)
                    if s == 0:
                        sp.wait_ge(sort_s.rest_out, 16)
                sp.nop(nofuse=True)
                for f, c in ((ef, EF), (et, ET), (stf, STF)):
                    v = f[0:P * COLS].rearrange("(p c) d -> p c d", p=P)
                    sp.dma_start(prow[:, s, :, c:c + D], v[:, bass.ds((2 * use + s) * PB, PB), :]).then_inc(q.load[s], 16)

            def load_rest(q):
                sp.wait_ge(q.out[0], SORTED)
                for f, c in ((ef, EF), (et, ET), (stf, STF)):
                    sp.dma_start(prow[0:REST, 0, 0, c:c + D], f[P * COLS:E, :]).then_inc(q.rest_load, 16)

            for s in range(2):
                load(sort_s, s, 0)
            sp.wait_ge(s_clear_at, 1)
            with sp.Fori(0, (CLEARS + 1) // 2) as i:
                clear(sp, "s", sorted_s, 2 * i)
            with sp.Fori(1, PBATCHES // 4 + 1) as i:
                for s in range(2):
                    load(sort_s, s, i)
            sp.wait_ge(s_clear_at, 2)
            with sp.Fori(PBATCHES // 4 + 1, PBATCHES // 2) as i:
                for s in range(2):
                    load(sort_s, s, i)
                    for c in range(1 + s):
                        clear(sp, "d", sorted_d, 3 * i + (s + c - 3 * (PBATCHES // 4 + 1)))
            with sp.Fori(0, BULKS) as i:
                clear_bulk(sp, "d", sorted_d, i)
            load_rest(sort_s)

            def fetch(q):
                def body(i, s, first):
                    n = SLOTS * i + s
                    if not first:
                        sp.wait_ge(q.mm, (n - SLOTS + 1) * B)
                        sp.nop(nofuse=True)
                        if q is seg1:
                            sp.wait_ge(q.tab, 2 * (n - SLOTS + 1))
                    sp.nop(nofuse=True)
                    sp.dma_start(rows[:, s], q.table_rows[0:ROWS].rearrange("(c p) w -> p c w", p=P)[
                        :, bass.ds(n * B, B), :]).then_inc(q.row[s], 16)
                return body

            def fetch_sums(q, i, u, by="sd"):
                for t in range(NT):
                    at = {k: sp.value_load(lastrow[k][0:1, bass.ds(i * NT + t, 1)], min_val=0, max_val=CHUNKS * P)
                          for k in by if k in {k for _, k, _ in q.sums}}
                    for running, k, bufs in q.sums:
                        if k not in by:
                            continue
                        sp.dma_start(bufs[u][:, t, :], running[bass.ds(at[k], P), :]).then_inc(q.sum[u], 16)

            for q in plan:
                if isinstance(q, Pass):
                    if q is seg1:
                        for s in range(2):
                            sp.wait_ge(sort_s.out[s], SORTED)
                        sp.wait_ge(sort_s.rest_out, 16)
                        for s in range(SLOTS):
                            fetch(seg1)(0, s, True)
                    if q is seg4:
                        load_rest(sort_d)
                        for s in range(2):
                            sp.wait_ge(sort_d.out[s], SORTED)
                        sp.wait_ge(sort_d.rest_out, 16)
                        for s in range(SLOTS):
                            fetch(seg5)(0, s, True)
                    if q.wide:
                        with sp.Fori(1, BATCHES // SLOTS) as i:
                            for s in range(SLOTS):
                                fetch(q)(i, s, False)
                    else:
                        with sp.Fori(1, BATCHES // SLOTS) as i:
                            for half in range(2):
                                store(sp, q, i - 1, half)
                        for half in range(2):
                            store(sp, q, BATCHES // SLOTS - 1, half)
                    continue
                if q is not node4:
                    ahead(q, load)
                if q is node4:
                    for g in (seg1, seg4):
                        for s in range(2):
                            sp.wait_ge(g.out[s], HALVES * 16)
                    fetch_sums(q, 0, 0, "s")
                for s in range(2):
                    sp.wait_ge({1: seg1, 2: seg2, 3: seg3, 4: seg5}[q.number].out[s], HALVES * 16)
                if q is not node4:
                    if q is node1:
                        sp.wait_ge(s_last, 2)
                    fetch_sums(q, 0, 0)
                    view = h_dram[q.number].rearrange("(t p) d -> p t d", p=P)

                    def group(i, full):
                        if q is node3:
                            xs = x[0:N_FULL * P].rearrange("(t p) d -> p t d", p=P)
                            if full:
                                if not is_first(i):
                                    sp.wait_ge(node3.done, i)
                                    sp.nop(nofuse=True)
                                sp.dma_start(xres[:, :, :], xs[:, bass.ds(i * NT, NT), :]).then_inc(s_xload, 16)
                            else:
                                sp.wait_ge(s_hpad, 2)
                                sp.dma_start(xres[:, 0:NT - 1, :], xs[:, N_FULL - NT + 1:N_FULL, :]).then_inc(s_xload, 16)
                                sp.dma_start(xres[0:N_LAST, NT - 1, :], x[N_FULL * P:N, :]).then_inc(s_xload, 16)
                        if full:
                            sp.wait_ge(q.cat, i + 1)
                            sp.nop(nofuse=True)
                            fetch_sums(q, i + 1, 0)
                        beside(q, i, range(4), load)
                        sp.wait_ge(q.done, i + 1)
                        sp.nop(nofuse=True)
                        sp.dma_start(view[:, bass.ds(i * NT, NT), :], h[:, bass.ds(i * NT, NT), :]).then_inc(q.out, 16)
                    group(0, True)
                    with sp.Fori(1, NGROUPS - 1) as i:
                        group(i, True)
                    group(NGROUPS - 1, False)
                    if q is node3:
                        tail(load)
                else:
                    full = out[0:N_FULL * P].rearrange("(t p) d -> p t d", p=P)

                    def store_out(i):
                        sp.wait_ge(q.done, i + 1)
                        sp.nop(nofuse=True)
                        sp.dma_start(full[:, bass.ds(i * NT, NT), :], h[:, bass.ds(i * NT, NT), :]).then_inc(q.out, 16)
                    fetch_sums(q, 0, 0, "d")
                    fetch_sums(q, 1, 1)
                    with sp.Fori(0, NGROUPS // 2 - 1) as half:
                        for u in range(2):
                            sp.wait_ge(q.cat2, 2 * half + (u + 1))
                            sp.nop(nofuse=True)
                            fetch_sums(q, 2 * half + (u + 2), u)
                            store_out(2 * half + u)
                    store_out(NGROUPS - 2)
                    sp.wait_ge(q.done, NGROUPS)
                    t0 = (NGROUPS - 1) * NT
                    sp.dma_start(full[:, t0:N_FULL, :], h[:, t0:N_FULL, :]).then_inc(q.out, 16)
                    sp.dma_start(out[N_FULL * P:N, :], h[0:N_LAST, N_FULL, :]).then_inc(q.out, 16)
                    sp.wait_ge(q.out, (NGROUPS + 1) * 16)

        @block.gpsimd
        def _(pool):
            pool.iota(iota_tmp[:, 0:P], [[1, P]], base=0, channel_multiplier=0).then_inc(s_iota, 1)
            pool.iota(iota_part_i[:, :], [[0, 1]], base=0, channel_multiplier=1).then_inc(s_iota, 1)
            pool.iota(iota_mark[:, :], [[1, MARKS]], base=0, channel_multiplier=0).then_inc(s_iota, 1)
            pool.iota(iota_clear_i[:, :], [[1, CLEARS]], base=0, channel_multiplier=0).then_inc(s_iota, 1)

            def scatter(q, s, use):
                pool.wait_ge(q.load[s], use * 48 + 48)
                pool.wait_ge(q.meta[s], use * 3 + 3)
                pool.nop(nofuse=True)
                for j in range(PB):
                    pool.indirect_dma_start(
                        out=q.table, out_offset=bass.IndirectOffsetOnAxis(ap=ppos[:, s, j:j + 1], axis=0),
                        in_=prow[:, s, j, :], in_offset=None).then_inc(q.out[s], 16)

            def scatter_rest(q):
                pool.wait_ge(q.rest_load, 48)
                pool.wait_ge(q.rest_meta, 3)
                pool.nop(nofuse=True)
                pool.indirect_dma_start(
                    out=q.table, out_offset=bass.IndirectOffsetOnAxis(ap=ppos[0:REST, 0, 0:1], axis=0),
                    in_=prow[0:REST, 0, 0, :], in_offset=None).then_inc(q.rest_out, 16)

            pool.wait_ge(s_zrow["s"], (CLEARS + BULKS + 5) * 16)
            sort_batches(pool, sort_s, scatter)
            scatter_rest(sort_s)

            def gather(q):
                def body(i, s, first):
                    n = SLOTS * i + s
                    if q.wide:
                        pool.wait_ge(q.row[s], (i + 1) * 16)
                    else:
                        pool.wait_ge(q.idx, n + 1)
                    if not first:
                        pool.wait_ge(q.mm, (n - SLOTS + 1) * B)
                    elif q is seg5:
                        pool.wait_ge(seg4.mm, CHUNKS - (SLOTS - 1 - s) * B)
                    pool.nop(nofuse=True)
                    for b in range(B):
                        ap = rows[:, s, b, OTHER:OTHER + 1].bitcast(I32) if q.wide else gidx[:, s, b:b + 1]
                        pool.indirect_dma_start(
                            out=got[:, s, b, :], out_offset=None, in_=q.table,
                            in_offset=bass.IndirectOffsetOnAxis(ap=ap, axis=0)).then_inc(q.got[s], 16)
                return body

            prev = None
            for q in plan:
                if isinstance(q, Pass):
                    if q is seg4:
                        scatter_rest(sort_d)
                    if isinstance(prev, Nodes):
                        pool.wait_ge(prev.out, NGROUPS * 16)
                    batches(pool, gather(q))
                else:
                    if q is node1:
                        pool.wait_ge(s_zrow["d"], (CLEARS + BULKS) * 16)
                    if q is not node4:
                        ahead(q, scatter)
                        with pool.Fori(0, NGROUPS - 1) as i:
                            beside(q, i, range(4), scatter)
                        beside(q, NGROUPS - 1, range(4), scatter)
                        if q is node3:
                            tail(scatter)
                prev = q

        @block.tensor
        def _(pe):
            pe.wait_ge(s_const, 2)
            for n in range(2):
                base = 2 * STEPS * n

                def histogram(j, u, start):
                    pe.wait_ge(s_oh, j + (base + 1))
                    pe.matmul(ps_seg[:, 3 * (u % 2), 0:LANES * BINS], ones_bf[:, :], onehot[:, u], start=start,
                              stop=False, skip_group_check=True).then_inc(s_mul, 1)
                for u in range(4):
                    histogram(u, u, u < 2)
                with pe.Fori(1, STEPS // 4) as j:
                    for u in range(4):
                        histogram(4 * j + u, u, False)
                histogram(STEPS - 1, 0, False)
                pe.wait_ge(s_lane0, n + 1)
                for c in range(2):
                    pe.matmul(ps_seg[:, 1 + c, 0:LANES * BINS], ones[0:1, :], lane0[0:1, c], start=True,
                              stop=False, skip_group_check=True)

                def prefix(j, u):
                    pe.wait_ge(s_oh, j + (base + STEPS + 1))
                    pe.matmul(ps_seg[:, 1 + u % 2, 0:LANES * BINS], upper[:, :], onehot[:, u], start=False,
                              stop=False, skip_group_check=True).then_inc(s_rank, 1)

                def advance(j, u):
                    pe.wait_ge(s_read, j + (STEPS * n + 1))
                    pe.matmul(ps_seg[:, 1 + u % 2, 0:LANES * BINS], lower[:, :], onehot[:, u], start=False,
                              stop=False, skip_group_check=True).then_inc(s_mul, 1)
                for u in range(2):
                    prefix(u, u)
                with pe.Fori(0, STEPS // 4 - 1) as j:
                    for u in range(4):
                        advance(4 * j + u, u)
                        prefix(4 * j + (u + 2), (u + 2) % 4)
                for j in range(STEPS - 5, STEPS):
                    advance(j, j % 4)
                    if j + 2 < STEPS:
                        prefix(j + 2, (j + 2) % 4)
                pe.wait_ge(s_starts, n + 1)
                for a in range(4):
                    mm = pe.matmul(ps_seg[:, a, 0:MARKS], ones[0:T, :], starts[0:T, a, :], start=True, stop=True)
                mm.then_inc(s_bc, 1)
                pe.wait_ge(s_keep, n + 1)

            def seg(q):
                def body(i, s, first):
                    n = SLOTS * i + s
                    pe.wait_ge(q.oh, n + 1)
                    pe.wait_ge(q.got[s], (i + 1) * (16 * B))
                    for b in range(B):
                        if not (first and s == 0):
                            pe.wait_ge(q.run, n * B + (b - B + 1))
                        lhs = seg_oh[:, s, b, :]
                        if q.wide:
                            pe.matmul(ps_seg[:, b, 0:FEAT], lhs, rows[:, s, b, 0:FEAT], start=True, stop=True)
                            mm = pe.matmul(ps_seg[:, b, FEAT:WIDE], lhs, got[:, s, b, :], start=True, stop=True)
                        else:
                            mm = pe.matmul(ps_seg[:, b, 0:D], lhs, got[:, s, b, :], start=True, stop=True)
                        mm.then_inc(q.mm, 1)
                return body

            def layer(q):
                w = wts[q.number - 1]
                with pe.Fori(0, NGROUPS) as i:
                    pe.wait_ge(q.cat, i + 1)
                    for t in range(NT):
                        mm = pe.transpose(ps_t[:, t, :], cat[:, t, :], ident[:, :])
                    mm.then_inc(q.tr, 1)
                    pe.wait_ge(q.ct, i + 1)
                    for t in range(NT):
                        mm = pe.matmul(ps_o[:, t, :], catT[:, t, :], w[:, :], start=True, stop=True)
                    mm.then_inc(q.mm, 1)

            def last(q):
                def first_products(i, u):
                    pe.wait_ge(q.cat, i + 1)
                    for t in range(NT):
                        mm = pe.transpose(ps_t[:, t, :], cats[u][:, t, :], ident[:, :])
                    mm.then_inc(q.tr, 1)
                    pe.wait_ge(q.ct, i * 3 + 1)
                    pe.wait_ge(q.cat2, i + 1)
                    for t in range(NT):
                        mm = pe.transpose(ps_t[:, t, :], cats2[u][:, t, :], ident[:, :])
                    mm.then_inc(q.tr, 1)
                    pe.wait_ge(q.ct, i * 3 + 2)
                    for t in range(NT):
                        pe.matmul(products[u][:, t, :], cat2T[:, t, :], w_n2[:, :], start=True, stop=False,
                                  skip_group_check=True)
                        mm = pe.matmul(products[u][:, t, 0:D], catT[:, t, :], w_n1[:, :], start=False, stop=True,
                                       skip_group_check=True)
                    mm.then_inc(q.mm, 1)

                def last_product(i, u):
                    pe.wait_ge(q.cat3, i + 1)
                    for t in range(NT):
                        mm = pe.transpose(ps_t[:, t, :], cats[u][:, t, :], ident[:, :])
                    mm.then_inc(q.tr, 1)
                    pe.wait_ge(q.ct, i * 3 + 3)
                    for t in range(NT):
                        mm = pe.matmul(products[u][:, t, 0:D], catT[:, t, :], w_n3[:, :], start=True, stop=True)
                    mm.then_inc(q.mm, 1)

                first_products(0, 0)
                with pe.Fori(0, NGROUPS // 2 - 1) as half:
                    for u in range(2):
                        last_product(2 * half + u, u)
                        first_products(2 * half + (u + 1), 1 - u)
                last_product(NGROUPS - 2, 0)
                first_products(NGROUPS - 1, 1)
                last_product(NGROUPS - 1, 1)

            for q in plan:
                if isinstance(q, Pass):
                    if q is seg5:
                        pe.wait_ge(seg4.run, CHUNKS)
                    batches(pe, seg(q))
                elif q is node4:
                    last(q)
                else:
                    if q is node1:
                        pe.wait_ge(s_wload, 16 * 19)
                    layer(q)

        @block.scalar
        def _(act):
            act.wait_ge(s_const, 2)
            for n, (wg, wl, ws, bb) in enumerate(((Wg1, Wl1, Ws1, b1), (Wg2, Wl2, Ws2, b2), (Wgo, Wlo, Wso, bo))):
                act.dma_start(wts[n][0:D, 0:D], wg).then_inc(s_wload, 16)
                act.dma_start(wts[n][0:D, D:P], ws).then_inc(s_wload, 16)
                act.dma_start(wts[n][D:P, D:P], wl).then_inc(s_wload, 16)
                act.dma_start(bias[n][:, :], bb.unsqueeze(0).to_broadcast([P, D])).then_inc(s_wload, 16)
            act.dma_start(w_n1[:, :], W1t[0:2 * D, :]).then_inc(s_wload, 16)
            act.dma_start(w_n2[0:D, 0:D], W1t[2 * D:3 * D, :]).then_inc(s_wload, 16)
            act.dma_start(w_n2[D:P, D:P], W2t[2 * D:3 * D, :]).then_inc(s_wload, 16)
            act.dma_start(w_n3[:, :], W2t[0:2 * D, :]).then_inc(s_wload, 16)
            act.dma_start(bias_n1[:, :], c1.unsqueeze(0).to_broadcast([P, D])).then_inc(s_wload, 16)
            act.dma_start(bias_n2[:, :], c2.unsqueeze(0).to_broadcast([P, D])).then_inc(s_wload, 16)
            act.dma_start(unit[:, :], stf[0:1, :].to_broadcast([P, D])).then_inc(s_wload, 16)

            def meta(q, s, use):
                if not is_first(use):
                    act.wait_ge(q.out[s], use * (PB * 16))
                elif q is sort_d:
                    act.wait_ge(sort_s.out[s], SORTED)
                    if s == 0:
                        act.wait_ge(sort_s.rest_out, 16)
                cols = bass.ds((2 * use + s) * PB, PB)
                act.copy(prow[:, s, :, LOC], place[q.key][:, cols]).then_inc(q.meta[s], 1)
                act.copy(prow[:, s, :, OTHER].bitcast(I32), keys[q.other][:, cols]).then_inc(q.meta[s], 1)
                act.copy(ppos[:, s, :], pos[q.key][:, cols]).then_inc(q.meta[s], 1)

            def meta_rest(q):
                act.wait_ge(q.out[0], SORTED)
                act.copy(prow[0:REST, 0, 0, LOC:LOC + 1], place[q.key][0:REST, COLS:COLS + 1]).then_inc(q.rest_meta, 1)
                act.copy(prow[0:REST, 0, 0, OTHER:OTHER + 1].bitcast(I32),
                         keys[q.other][0:REST, COLS:COLS + 1]).then_inc(q.rest_meta, 1)
                act.copy(ppos[0:REST, 0, 0:1], pos[q.key][0:REST, COLS:COLS + 1]).then_inc(q.rest_meta, 1)

            act.wait_ge(s_clear_at, 1)
            with act.Fori(0, CLEARS // 2) as i:
                clear(act, "s", sorted_s, 2 * i + 1)
            with act.Fori(0, BULKS) as i:
                clear_bulk(act, "s", sorted_s, i)
            act.wait_ge(s_load["d"], 32)
            for s in range(2):
                if s == 0:
                    act.wait_ge(s_prod, AHEAD)
                meta(sort_s, s, 0)
            with act.Fori(1, STEPS // AHEAD) as i:
                act.wait_ge(s_prod, i * AHEAD + AHEAD)
                for s in range(2):
                    meta(sort_s, s, i)
            act.wait_ge(s_prod, STEPS)
            with act.Fori(STEPS // AHEAD, PBATCHES // 2) as i:
                for s in range(2):
                    meta(sort_s, s, i)
            meta_rest(sort_s)
            act.wait_ge(s_hpad, 1)
            act.dma_start(h[:, 0:N_FULL, :], x[0:N_FULL * P].rearrange("(t p) d -> p t d", p=P)).then_inc(s_xload, 16)
            act.dma_start(h[0:N_LAST, N_FULL, :], x[N_FULL * P:N, :]).then_inc(s_xload, 16)
            def keep_idx(q):
                def body(i, s, first):
                    n = SLOTS * i + s
                    act.wait_ge(q.row[s], (i + 1) * 16)
                    act.copy(loc_s[:, bass.ds(n * B, B)], rows[:, s, :, LOC]).then_inc(q.tab, 1)
                    act.copy(id_d[:, bass.ds(n * B, B)], rows[:, s, :, OTHER].bitcast(I32)).then_inc(q.tab, 1)
                return body

            def place_idx(q):
                def body(i, s, first):
                    n = SLOTS * i + s
                    if not first:
                        act.wait_ge(q.got[s], i * (16 * B))
                    act.copy(gidx[:, s, :], id_d[:, bass.ds(n * B, B)]).then_inc(q.idx, 1)
                return body

            def transposed(q, i, c, copies):
                act.wait_ge(q.tr, i * copies + (c + 1))
                to = cat2T if c == 1 else catT
                act.copy(to[:, 0:4, :], ps_t[:, 0:4, :])
                act.copy(to[:, 4:NT, :], ps_t[:, 4:NT, :]).then_inc(q.ct, 1)

            def root(q, i, nm=nm):
                act.wait_ge(q.var, i + 1)
                act.activation(nm[:, :, 2], nm[:, :, 1], ACT.Sqrt).then_inc(q.std, 1)

            for q in plan:
                if isinstance(q, Pass):
                    if q.wide:
                        keep = keep_idx(q) if q is seg1 else None
                        if keep:
                            for s in range(SLOTS):
                                keep(0, s, True)
                        with act.Fori(1, BATCHES // SLOTS) as i:
                            for half in range(2):
                                store(act, q, i - 1, half)
                                if keep:
                                    keep(i, 2 * half, False)
                                    keep(i, 2 * half + 1, False)
                        for half in range(2):
                            store(act, q, BATCHES // SLOTS - 1, half)
                        if keep:
                            act.wait_ge(q.tab, 2 * BATCHES)
                    elif not q.wide:
                        if q is seg4:
                            meta_rest(sort_d)
                        batches(act, place_idx(q))
                elif q is not node4:
                    if q is node1:
                        act.wait_ge(s_ranked, 2)
                    ahead(q, meta)

                    def group(i):
                        beside(q, i, range(2), meta)
                        transposed(q, i, 0, 1)
                        act.wait_ge(q.neg, i + 1)
                        act.activation(nb[:, :, :], nb[:, :, :], ACT.Exp).then_inc(q.exp, 1)
                        if q is node3:
                            root(q, i)
                        beside(q, i, range(2, 4), meta)
                    with act.Fori(0, NGROUPS - 1) as i:
                        group(i)
                    group(NGROUPS - 1)
                    if q is node3:
                        tail(meta)
                else:
                    for c in range(2):
                        transposed(q, 0, c, 3)

                    def group_beside_next(i, u):
                        transposed(q, i, 2, 3)
                        for c in range(2):
                            transposed(q, i + 1, c, 3)
                        root(q, i, nms[u])
                    with act.Fori(0, NGROUPS // 2 - 1) as half:
                        for u in range(2):
                            group_beside_next(2 * half + u, u)
                    group_beside_next(NGROUPS - 2, 0)
                    transposed(q, NGROUPS - 1, 2, 3)
                    root(q, NGROUPS - 1, nms[1])

        @block.vector
        def _(dve):
            dve.memset(zeros[:, :], 0.0).then_inc(s_zero, 1)
            for k in "sd":
                dve.memset(keys[k][:, COLS:KEYC], T * P).then_inc(s_pad, 1)
            dve.wait_ge(s_pad, 2)
            dve.memset(prow[:, :, :, ONE:ONE + 1], 1.0)
            dve.memset(prow[:, :, :, OTHER + 1:ROW], 0.0).then_inc(s_const, 1)
            dve.memset(ones_bf[:, :], 1.0)
            dve.memset(ones[:, :], 1.0)
            for wmat in (*wts, w_n2):
                dve.memset(wmat[:, :], 0.0)
            dve.memset(loc_s[:, CHUNKS:CHUNKS + B], 0.0)
            dve.memset(run[:, :, :, :], 0.0)
            dve.wait_ge(s_iota, 4)
            dve.tensor_copy(iota_part[:, :], iota_part_i[:, :])
            dve.tensor_scalar(own[:, :], iota_clear_i[:, :], float(CHUNKS + BULKS * BULK), None, ALU.add)
            chain(dve, dve.tensor_copy(iota_row[:, :], iota_tmp[:, :]))
            dve.tensor_copy(bin_lane[:, :, :], iota_tmp[:, 0:BINS].unsqueeze(2).to_broadcast([P, BINS, LANES]))
            dve.tensor_scalar(iota_loc[:, :], iota_row[:, :], 1.0, None, ALU.add)
            dve.tensor_scalar(ident[:, :], iota_row[:, :], iota_part[:, 0:1], None, ALU.is_equal)
            dve.tensor_scalar(upper[:, :], iota_row[:, :], iota_part[:, 0:1], None, ALU.is_gt)
            dve.tensor_scalar(lower[:, :], iota_row[:, :], iota_part[:, 0:1], None, ALU.is_le).then_inc(s_const, 1)
            dve.wait_ge(s_const, 2)

            def bins_of(j, p):
                dve.tensor_tensor(
                    onehot[:, p], tid[:, bass.ds(j * LANES, LANES)].unsqueeze(1).to_broadcast([P, BINS, LANES]),
                    bin_lane[:, :, :], ALU.is_equal).then_inc(s_oh, 1)

            def ranking(n, k):
                base = 2 * STEPS * n
                dve.wait_ge(s_load[k], 32)
                chain(dve, dve.tensor_scalar(bits[:, :], keys[k][:, :], P - 1, None, ALU.bitwise_and))
                chain(dve, dve.tensor_scalar(place[k][:, :], bits[:, :], 1.0, None, ALU.add))
                chain(dve, dve.tensor_scalar(bits[:, :], keys[k][:, :], 7, None, ALU.logical_shift_right))
                chain(dve, dve.tensor_copy(tid[:, :], bits[:, :]))

                for j in range(4):
                    bins_of(j, j)

                def more(j, u):
                    dve.wait_ge(s_mul, j + (base - 3))
                    bins_of(j, u)
                with dve.Fori(1, STEPS // 4) as j:
                    for u in range(4):
                        more(4 * j + u, u)
                more(STEPS - 1, 0)
                dve.wait_ge(s_mul, base + STEPS)
                for c in range(2):
                    ins = dve.tensor_copy(prod[:, c], ps_seg[:, 3 * c, 0:LANES * BINS].rearrange("p (b l) -> p b l", l=LANES))
                    chain(dve, ins)
                chain(dve, dve.tensor_reduce(count[:, :], prod[:, 0], AX.X, ALU.add))
                chain(dve, dve.tensor_reduce(binsq[:, :], prod[:, 1], AX.X, ALU.add))
                chain(dve, dve.tensor_tensor(count[:, :], count[:, :], binsq[:, :], ALU.add))
                chain(dve, dve.tensor_scalar(nchunk_i[:, :], count[:, :], float(P - 1), None, ALU.add))
                chain(dve, dve.tensor_scalar(nchunk_i[:, :], nchunk_i[:, :], 7, None, ALU.logical_shift_right))
                chain(dve, dve.tensor_copy(nchunk[:, :], nchunk_i[:, :]))
                chain(dve, dve.tensor_tensor_scan(cend[:, :], nchunk[:, :], nchunk[:, :], 0.0, ALU.add, ALU.bypass))
                chain(dve, dve.tensor_tensor(cstart[:, :], cend[:, :], nchunk[:, :], ALU.subtract))
                chain(dve, dve.tensor_scalar(filled[:, :], nchunk[:, :], 1.0, None, ALU.min))
                chain(dve, dve.memset(block_in[:, :], 0.0))
                chain(dve, dve.memset(block_at[:, :], 0.0))
                chain(dve, dve.tensor_copy(block_in[:, 0:T], filled[:, 0:T]))
                chain(dve, dve.tensor_scalar(block_at[:, 0:T], cend[:, 0:T], 1.0, None, ALU.subtract))
                chain(dve, dve.tensor_tensor(block_at[:, :], block_at[:, :], own[:, :], ALU.subtract))
                chain(dve, dve.tensor_tensor(block_at[:, :], block_at[:, :], block_in[:, :], ALU.mult))
                chain(dve, dve.tensor_tensor(block_at[:, :], block_at[:, :], own[:, :], ALU.add))
                chain(dve, dve.tensor_scalar(clear_at[k][:, :], block_at[:, :], float(P), None, ALU.mult))
                chain(dve, dve.tensor_scalar(bulk_first[:, :], iota_clear_i[:, 0:BULKS], float(BULK), cend[:, T - 1:T],
                                             ALU.mult, ALU.add))
                dve.tensor_scalar(bulk_at[k][:, :], bulk_first[:, :], float(P), None, ALU.mult).then_inc(s_clear_at, 1)
                chain(dve, dve.tensor_scalar(lane0[:, 0, :, 0], cstart[:, :], float(P), None, ALU.mult))
                for l in range(1, 2 * LANES):
                    (c, m), (c0, m0) = divmod(l, LANES), divmod(l - 1, LANES)
                    ins = dve.tensor_tensor(lane0[:, c, :, m], lane0[:, c0, :, m0], prod[:, c0, :, m0], ALU.add)
                    if l < 2 * LANES - 1:
                        chain(dve, ins)
                ins.then_inc(s_lane0, 1)
                dve.wait_ge(s_lane0, n + 1)

                def position(j, u, more=True):
                    dve.wait_ge(s_rank, j + (STEPS * n + 1))
                    if isinstance(j, int) and j < 2 and n == 0:
                        pass
                    else:
                        dve.wait_ge(s_prod, j + (STEPS * n - 1))
                    dve.tensor_tensor(prod[:, u % 2], onehot[:, u],
                                      ps_seg[:, 1 + u % 2, 0:LANES * BINS].rearrange("p (b l) -> p b l", l=LANES),
                                      ALU.mult).then_inc(s_read, 1)
                    if more:
                        dve.wait_ge(s_mul, j + (base + STEPS))
                        bins_of(j + 3, (u + 3) % 4)
                    dve.wait_ge(s_read, j + (STEPS * n + 1))
                    dve.tensor_reduce(pos[k][:, bass.ds(j * LANES, LANES)], prod[:, u % 2].rearrange("p b l -> p l b"),
                                      AX.X, ALU.add).then_inc(s_prod, 1)
                for j in range(3):
                    bins_of(j, j)
                for u in range(4):
                    position(u, u)
                with dve.Fori(1, STEPS // 4 - 1) as j:
                    for u in range(4):
                        position(4 * j + u, u)
                for j in range(STEPS - 5, STEPS):
                    position(j, j % 4, j + 3 < STEPS)
                dve.wait_ge(s_prod, STEPS * (n + 1))
                dve.wait_ge(s_mul, base + 2 * STEPS)
                dve.memset(binsq[:, :], 0.0).then_inc(s_ranked, 1)
                dve.wait_ge(s_ranked, n + 1)

                for row, col in ((cstart, startcol), (filled, fillcol)):
                    chain(dve, dve.tensor_tensor(binsq[:, :], row[:, :], ident[:, 0:BINS], ALU.mult))
                    chain(dve, dve.tensor_reduce(col[:, :], binsq[:, :], AX.X, ALU.add))
                for a in range(4):
                    dve.tensor_scalar(starts[:, a, :], iota_mark[:, :], float(MARKS * a), startcol[:, 0:1],
                                      ALU.add, ALU.is_equal).then_inc(s_v, 1)
                vcount[0] += 4
                dve.wait_ge(s_v, vcount[0])
                dve.tensor_scalar(starts[:, :, :], starts[:, :, :], fillcol[:, 0:1], None, ALU.mult).then_inc(s_starts, 1)
                dve.wait_ge(s_bc, n + 1)
                dve.tensor_scalar(keep[k][:, :].rearrange("p (a c) -> p a c", a=4), ps_seg[:, :, 0:MARKS],
                                  -1.0, 1.0, ALU.mult, ALU.add).then_inc(s_keep, 1)
                chain(dve, dve.tensor_tensor(binsq[:, :], cend[:, :], filled[:, :], ALU.mult))
                dve.tensor_scalar(lastrow[k][:, :], binsq[:, 0:T], float(P), None, ALU.mult).then_inc(s_last, 1)

            ranking(0, "s")
            ranking(1, "d")
            dve.wait_ge(s_clear_at, 2)
            dve.wait_ge(s_last, 2)
            dve.memset(h[:, N_FULL, :], 0.0).then_inc(s_hpad, 1)
            dve.wait_ge(s_hpad, 1)

            def onehots(q, i, s, first):
                n = SLOTS * i + s
                if not first:
                    dve.wait_ge(q.mm, (n - SLOTS + 1) * B)
                if q.wide:
                    dve.wait_ge(q.row[s], (i + 1) * 16)
                    loc = rows[:, s, :, LOC:LOC + 1]
                else:
                    loc = loc_s[:, bass.ds(n * B, B)].unsqueeze(2)
                dve.tensor_tensor(seg_oh[:, s], loc.to_broadcast([P, B, P]),
                                  iota_loc[:, :].unsqueeze(1).to_broadcast([P, B, P]),
                                  ALU.is_equal).then_inc(q.oh, 1)

            def running(q, i, s, first):
                n = SLOTS * i + s
                w = q.width
                half, at = s // 2, (s % 2) * B
                if s % 2 == 0 and not first:
                    dve.wait_ge(q.out[half], i * 16)
                for b in range(B):
                    dve.wait_ge(q.mm, n * B + (b + 1))
                    if not (first and s == 0 and b == 0):
                        dve.wait_ge(q.run, n * B + b)
                    before = run[:, half, at + b - 1, 0:w] if at + b else run[:, 1 - half, 2 * B - 1, 0:w]
                    dve.scalar_tensor_tensor(
                        run[:, half, at + b, 0:w], before, keep[q.key][:, bass.ds(n * B + b, 1)],
                        ps_seg[:, b, 0:w], ALU.mult, ALU.add).then_inc(q.run, 1)

            def seg(q):
                def body(i, first, last):
                    for s in range(SLOTS):
                        if s < SLOTS - 1:
                            onehots(q, i, s + 1, first)
                        elif not last:
                            onehots(q, i + 1, 0, False)
                        running(q, i, s, first)
                onehots(q, 0, 0, True)
                body(0, True, False)
                with dve.Fori(1, BATCHES // SLOTS - 1) as i:
                    body(i, False, False)
                body(BATCHES // SLOTS - 1, False, True)

            def bc(ap):
                return ap.unsqueeze(2).to_broadcast([P, NT, D])

            class Steps:

                def __init__(self, signal, i, per):
                    self.chain, self.i, self.per, self.n = signal, i, per, 0

                def __call__(self, ins):
                    self.n += 1
                    ins.then_inc(self.chain, 1)
                    dve.wait_ge(self.chain, self.i * self.per + self.n)

            def layernorm(q, step, i, na=na, nb=nb, nm=nm):
                hs = h[:, bass.ds(i * NT, NT), :]
                step(dve.tensor_reduce(nm[:, :, 0], na[:, :, :], AX.X, ALU.add))
                step(dve.tensor_scalar(nm[:, :, 0], nm[:, :, 0], 1.0 / D, None, ALU.mult))
                step(dve.tensor_tensor(na[:, :, :], na[:, :, :], bc(nm[:, :, 0]), ALU.subtract))
                step(dve.tensor_tensor(nb[:, :, :], na[:, :, :], na[:, :, :], ALU.mult))
                step(dve.tensor_reduce(nm[:, :, 1], nb[:, :, :], AX.X, ALU.add))
                dve.tensor_scalar(nm[:, :, 1], nm[:, :, 1], 1.0 / D, EPS, ALU.mult, ALU.add).then_inc(q.var, 1)
                dve.wait_ge(q.std, i + 1)
                step(dve.reciprocal(nm[:, :, 3], nm[:, :, 2]))
                dve.tensor_tensor(hs, na[:, :, :], bc(nm[:, :, 3]), ALU.mult).then_inc(q.done, 1)
                dve.wait_ge(q.done, i + 1)

            def layer(q):
                wide = q is node1
                normed = q is node3
                per = (4 if wide else 0) + 5 + (8 if normed else 0)
                def group(i):
                    step = Steps(q.v, i, per)
                    ts = bass.ds(i * NT, NT)
                    hs = h[:, ts, :]
                    dve.wait_ge(q.sum[0], (i + 1) * (16 * NT))
                    if wide:
                        step(dve.tensor_scalar(linked[:, ts], sum_a[:, :, ONE], 1.0, None, ALU.min))
                        step(dve.tensor_scalar(nm[:, :, 4], sum_a[:, :, ONE], 1.0, None, ALU.max))
                        step(dve.reciprocal(nm[:, :, 5], nm[:, :, 4]))
                        step(dve.tensor_scalar(inv[:, ts], nm[:, :, 5], 1.0, None, ALU.mult))
                        agg = sum_a[:, :, FEAT:WIDE]
                    else:
                        agg = sum_c[:, :, :]
                    step(dve.tensor_scalar(cat[:, :, 0:D], hs, 1.0, None, ALU.mult))
                    dve.tensor_tensor(cat[:, :, D:P], agg, bc(inv[:, ts]), ALU.mult).then_inc(q.cat, 1)
                    dve.wait_ge(q.mm, i + 1)
                    step(dve.tensor_tensor(na[:, :, :], ps_o[:, 0:NT, 0:D],
                                           bias[q.number - 1][:, :].unsqueeze(1).to_broadcast([P, NT, D]), ALU.add))
                    step(dve.tensor_tensor(nb[:, :, :], ps_o[:, 0:NT, D:P], bc(linked[:, ts]), ALU.mult))
                    step(dve.tensor_tensor(na[:, :, :], na[:, :, :], nb[:, :, :], ALU.add))
                    dve.tensor_scalar(nb[:, :, :], na[:, :, :], 0.0, None, ALU.min).then_inc(q.neg, 1)
                    step(dve.tensor_scalar(cat[:, :, 0:D], na[:, :, :], 0.0, -1.0, ALU.max, ALU.add))
                    dve.wait_ge(q.exp, i + 1)
                    if not normed:
                        dve.tensor_tensor(hs, cat[:, :, 0:D], nb[:, :, :], ALU.add).then_inc(q.done, 1)
                        dve.wait_ge(q.done, i + 1)
                    else:
                        step(dve.tensor_tensor(na[:, :, :], cat[:, :, 0:D], nb[:, :, :], ALU.add))
                        final = isinstance(i, int) and i == NGROUPS - 1
                        dve.wait_ge(s_xload, i * 16 + (64 if final else 48))
                        step(dve.tensor_tensor(na[:, :, :], na[:, :, :], xres[:, :, :], ALU.add))
                        layernorm(q, step, i)
                    assert step.n == per, step.n

                group(0)
                with dve.Fori(1, NGROUPS - 1) as i:
                    group(i)
                if normed:
                    dve.memset(xres[:, NT - 1, :], 0.0).then_inc(s_hpad, 1)
                group(NGROUPS - 1)

            def last(q):
                sums = list(zip(*(bufs for _, _, bufs in q.sums)))

                def front(i, half, u):
                    sum_a, sum_b, sum_c = sums[u]
                    cat, cat2, na, nb, nm = cats[u], cats2[u], nas[u], nbs[u], nms[u]
                    step = Steps(q.front, i, 7)
                    hs = h[:, bass.ds(i * NT, NT), :]
                    unit_t = unit[:, :].unsqueeze(1).to_broadcast([P, NT, D])
                    dve.wait_ge(q.sum[u], half * (16 * NT * 3) + 16 * NT * 3)
                    step(dve.tensor_tensor(na, sum_c[:, :, :], sum_b[:, :, FEAT:WIDE], ALU.add))
                    step(dve.tensor_tensor(cat[:, :, 0:D], na, hs, ALU.add))
                    step(dve.tensor_tensor(sum_a[:, :, 0:FEAT], sum_a[:, :, 0:FEAT], sum_b[:, :, 0:FEAT], ALU.add))
                    dve.tensor_copy(cat[:, :, D:P], sum_a[:, :, EF:EF + D]).then_inc(q.cat, 1)
                    step(dve.tensor_scalar(nm[:, :, 4], sum_a[:, :, ONE], 1.0, None, ALU.add))
                    step(dve.reciprocal(nm[:, :, 5], nm[:, :, 4]))
                    dve.tensor_tensor(cat2[:, :, 0:D], sum_a[:, :, ET:ET + D], unit_t, ALU.add)
                    step(dve.tensor_tensor(nb, sum_a[:, :, STF:STF + D], unit_t, ALU.add))
                    dve.tensor_tensor(cat2[:, :, D:P], nb, bc(nm[:, :, 5]), ALU.mult).then_inc(q.cat2, 1)
                    dve.wait_ge(q.cat2, i + 1)
                    step(dve.tensor_tensor(nb, bias_n1[:, :].unsqueeze(1).to_broadcast([P, NT, D]),
                                           bc(nm[:, :, 4]), ALU.mult))
                    assert step.n == 7, step.n

                def finish(i, u):
                    cat, na, nb, nm, ps = cats[u], nas[u], nbs[u], nms[u], products[u]
                    step = Steps(q.v, i, 11)
                    hs = h[:, bass.ds(i * NT, NT), :]
                    dve.wait_ge(q.mm, i * 2 + 1)
                    step(dve.tensor_tensor(na, ps[:, 0:NT, 0:D], nb, ALU.add))
                    step(dve.tensor_scalar(cat[:, :, D:P], hs, 1.0, None, ALU.mult))
                    dve.tensor_scalar(cat[:, :, 0:D], na, 0.0, None, ALU.max).then_inc(q.cat3, 1)
                    dve.wait_ge(q.mm, i * 2 + 2)
                    step(dve.tensor_tensor(na, ps[:, 0:NT, 0:D],
                                           bias_n2[:, :].unsqueeze(1).to_broadcast([P, NT, D]), ALU.add))
                    step(dve.tensor_tensor(na, na, ps[:, 0:NT, D:P], ALU.add))
                    step(dve.tensor_tensor(na, na, hs, ALU.add))
                    layernorm(q, step, i, na, nb, nm)
                    assert step.n == 11, step.n

                front(0, 0, 0)
                with dve.Fori(0, NGROUPS // 2 - 1) as half:
                    front(2 * half + 1, half, 1)
                    finish(2 * half, 0)
                    front(2 * half + 2, half + 1, 0)
                    finish(2 * half + 1, 1)
                front(NGROUPS - 1, NGROUPS // 2 - 1, 1)
                finish(NGROUPS - 2, 0)
                finish(NGROUPS - 1, 1)

            for q in plan:
                if isinstance(q, Pass):
                    if q is seg2:
                        dve.wait_ge(seg1.tab, 2 * BATCHES)
                    if q is seg5:
                        for s in range(2):
                            dve.wait_ge(seg4.out[s], HALVES * 16)
                    seg(q)
                elif q is node4:
                    last(q)
                else:
                    if q is node1:
                        dve.wait_ge(s_wload, 16 * 19)
                        dve.wait_ge(s_xload, 32)
                    layer(q)


_INS = ["x", "src", "dst", "edge_attr_64", "edge_attr_64_n2", "edge_attr_64_n3",
        "L0_gnn_Wg1", "L0_gnn_Wl1", "L0_gnn_Ws1", "L0_gnn_b1", "L0_gnn_Wg2", "L0_gnn_Wl2", "L0_gnn_Ws2", "L0_gnn_b2",
        "L0_gnn_Wgo", "L0_gnn_Wlo", "L0_gnn_Wso", "L0_gnn_bo", "L1_gnn_W1", "L1_gnn_b1", "L1_gnn_W2", "L1_gnn_b2"]


def kernel(**inputs):
    import concourse.bacc as bacc
    from concourse.bass_utils import run_bass_kernel_spmd

    nc = bacc.Bacc("TRN2", target_bir_lowering=False, num_devices=1)
    arrays, args = {}, []
    for name in _INS:
        a = np.asarray(inputs[name])
        if name in ("L1_gnn_W1", "L1_gnn_W2"):
            a = a.T
        a = np.ascontiguousarray(a)
        arrays[f"in_{name}"] = a
        args.append(nc.dram_tensor(f"in_{name}", a.shape, mybir.dt.from_np(a.dtype), kind="ExternalInput").ap())
    args.append(nc.dram_tensor("out_x", (N, D), F32, kind="ExternalOutput").ap())
    build(nc, *args)
    r = run_bass_kernel_spmd(nc, [arrays], core_ids=[0])
    return r.results[0]["out_x"]
```
